# Optimizing a Trainium2 kernel written in Bass

```python
import numpy as np
import jax
import jax.numpy as jnp

def _softmax(x, axis=-1):
    return jax.nn.softmax(x, axis=axis)

def _gelu(x):
    return jax.nn.gelu(x, approximate=True)

def _silu(x):
    return jax.nn.silu(x)

def _sigmoid(x):
    return jax.nn.sigmoid(x)

def _layernorm(x, axis=-1, eps=1e-05):
    m = jnp.mean(x, axis=axis, keepdims=True)
    v = jnp.var(x, axis=axis, keepdims=True)
    return (x - m) / jnp.sqrt(v + eps)

def _scatter_add(tgt, idx, src, axis=0):
    return tgt.at[idx].add(src)

def _segment_sum(src, seg, n):
    return jax.ops.segment_sum(src, seg, n)
kernel_name = 'mk_seq_preln_d1_jaxref_r4_7a7bfd'

def setup_inputs(seed: int=0):
    np.random.seed(seed)
    _w = jnp.asarray

    def _L0_attn_setup():
        import jax, jax.numpy as jnp
        import numpy as np
        DIM = 256
        DT_RANK = 64
        D_STATE = 16
        BATCH = 2
        SEQ = 512
        EPS = 1e-05

        def _selective_scan(u, delta, A, B, C, D):
            deltaA = jnp.exp(jnp.einsum('bld,dn->bldn', delta, A))
            deltaBu = jnp.einsum('bld,bln->bldn', delta * u, B)

            def step(h, inp):
                dA, dBu, Ct = inp
                h = dA * h + dBu
                y = jnp.einsum('bdn,bn->bd', h, Ct)
                return (h, y)
            h0 = jnp.zeros((u.shape[0], u.shape[2], A.shape[1]), u.dtype)
            xs = (jnp.moveaxis(deltaA, 1, 0), jnp.moveaxis(deltaBu, 1, 0), jnp.moveaxis(C, 1, 0))
            _, ys = jax.lax.scan(step, h0, xs)
            y = jnp.moveaxis(ys, 0, 1)
            return y + u * D

        def _ssm(u, deltaBC_W, dt_W, dt_b, A_log, D):
            A = -jnp.exp(A_log)
            dbc = u @ deltaBC_W.T
            delta = dbc[..., :DT_RANK]
            B = dbc[..., DT_RANK:DT_RANK + D_STATE]
            C = dbc[..., DT_RANK + D_STATE:]
            delta = jax.nn.softplus(delta @ dt_W.T + dt_b)
            return _selective_scan(u, delta, A, B, C, D)
        key = jax.random.key(seed)
        ks = jax.random.split(key, 8)
        s = 0.02
        x = jax.random.normal(ks[0], (BATCH, SEQ, DIM), jnp.float32)
        ln_w = jnp.ones((DIM,), jnp.float32)
        ln_b = jnp.zeros((DIM,), jnp.float32)
        proj_W = jax.random.normal(ks[1], (DIM, DIM), jnp.float32) * s
        proj_b = jnp.zeros((DIM,), jnp.float32)
        fconv_W = jax.random.normal(ks[2], (DIM, DIM), jnp.float32) * s
        fconv_b = jnp.zeros((DIM,), jnp.float32)
        bconv_W = jax.random.normal(ks[3], (DIM, DIM), jnp.float32) * s
        bconv_b = jnp.zeros((DIM,), jnp.float32)
        deltaBC_W = jax.random.normal(ks[4], (DT_RANK + 2 * D_STATE, DIM), jnp.float32) * s
        dt_W = jax.random.normal(ks[5], (DIM, DT_RANK), jnp.float32) * s
        dt_b = jnp.zeros((DIM,), jnp.float32)
        A_log = jnp.log(jnp.tile(jnp.arange(1, D_STATE + 1, dtype=jnp.float32)[None, :], (DIM, 1)))
        D = jnp.ones((DIM,), jnp.float32)
        return dict(x=x, ln_w=ln_w, ln_b=ln_b, proj_W=proj_W, proj_b=proj_b, fconv_W=fconv_W, fconv_b=fconv_b, bconv_W=bconv_W, bconv_b=bconv_b, deltaBC_W=deltaBC_W, dt_W=dt_W, dt_b=dt_b, A_log=A_log, D=D)
    _L0_attn_in = _L0_attn_setup()

    def _L0_ffn_setup():
        import jax, jax.numpy as jnp
        import numpy as np
        DIM = 256
        N_EXPERTS = 16
        TOP_K = 4
        N_GROUP = 4
        TOPK_GROUP = 2
        MOE_INTER = 128
        SHARED_INTER = 512
        ROUTED_SCALE = 2.5

        def relu2(x):
            return jnp.square(jax.nn.relu(x))

        def _router(x2, gate_w, bias_e):
            T = x2.shape[0]
            logits = x2 @ gate_w.T
            scores = jax.nn.sigmoid(logits)
            sc = jax.lax.stop_gradient(scores + bias_e[None, :])
            grp = sc.reshape(T, N_GROUP, N_EXPERTS // N_GROUP)
            top2, _ = jax.lax.top_k(grp, 2)
            group_scores = top2.sum(-1)
            _, gidx = jax.lax.top_k(group_scores, TOPK_GROUP)
            rows = jnp.arange(T)[:, None]
            gmask = jnp.zeros((T, N_GROUP), dtype=sc.dtype).at[rows, gidx].set(1.0)
            smask = jnp.repeat(gmask, N_EXPERTS // N_GROUP, axis=1)
            masked = jnp.where(smask > 0, sc, 0.0)
            _, topk_idx = jax.lax.top_k(masked, TOP_K)
            topk_w = jnp.take_along_axis(scores, topk_idx, axis=1)
            topk_w = topk_w / (topk_w.sum(-1, keepdims=True) + 1e-20)
            topk_w = topk_w * ROUTED_SCALE
            return (topk_idx, topk_w)
        key = jax.random.key(seed)
        ks = jax.random.split(key, 6)
        hidden_states = jax.random.normal(ks[0], (2, 512, DIM), dtype=jnp.float32)
        gate_w = jax.random.normal(ks[1], (N_EXPERTS, DIM), dtype=jnp.float32) * 0.02
        bias_e = jnp.zeros((N_EXPERTS,), dtype=jnp.float32)
        up_w = jax.random.normal(ks[2], (N_EXPERTS, MOE_INTER, DIM), dtype=jnp.float32) * 0.02
        down_w = jax.random.normal(ks[3], (N_EXPERTS, DIM, MOE_INTER), dtype=jnp.float32) * 0.02
        shared_up = jax.random.normal(ks[4], (SHARED_INTER, DIM), dtype=jnp.float32) * 0.02
        shared_down = jax.random.normal(ks[5], (DIM, SHARED_INTER), dtype=jnp.float32) * 0.02
        return {'hidden_states': hidden_states, 'gate_w': gate_w, 'bias_e': bias_e, 'up_w': up_w, 'down_w': down_w, 'shared_up': shared_up, 'shared_down': shared_down}
    _L0_ffn_in = _L0_ffn_setup()
    _d = {'L0_attn_x': _L0_attn_in['x'], 'L0_attn_ln_w': _L0_attn_in['ln_w'], 'L0_attn_ln_b': _L0_attn_in['ln_b'], 'L0_attn_proj_W': _L0_attn_in['proj_W'], 'L0_attn_proj_b': _L0_attn_in['proj_b'], 'L0_attn_fconv_W': _L0_attn_in['fconv_W'], 'L0_attn_fconv_b': _L0_attn_in['fconv_b'], 'L0_attn_bconv_W': _L0_attn_in['bconv_W'], 'L0_attn_bconv_b': _L0_attn_in['bconv_b'], 'L0_attn_deltaBC_W': _L0_attn_in['deltaBC_W'], 'L0_attn_dt_W': _L0_attn_in['dt_W'], 'L0_attn_dt_b': _L0_attn_in['dt_b'], 'L0_attn_A_log': _L0_attn_in['A_log'], 'L0_attn_D': _L0_attn_in['D'], 'L0_ffn_gate_w': _L0_ffn_in['gate_w'], 'L0_ffn_bias_e': _L0_ffn_in['bias_e'], 'L0_ffn_up_w': _L0_ffn_in['up_w'], 'L0_ffn_down_w': _L0_ffn_in['down_w'], 'L0_ffn_shared_up': _L0_ffn_in['shared_up'], 'L0_ffn_shared_down': _L0_ffn_in['shared_down']}
    _x0 = _d['L0_attn_x']
    _d['L0_attn_x'] = jax.random.normal(jax.random.fold_in(jax.random.key(seed), 1), (8, 512, 256), dtype=_x0.dtype)
    del _x0
    return _d

def reference(L0_attn_x, L0_attn_ln_w, L0_attn_ln_b, L0_attn_proj_W, L0_attn_proj_b, L0_attn_fconv_W, L0_attn_fconv_b, L0_attn_bconv_W, L0_attn_bconv_b, L0_attn_deltaBC_W, L0_attn_dt_W, L0_attn_dt_b, L0_attn_A_log, L0_attn_D, L0_ffn_gate_w, L0_ffn_bias_e, L0_ffn_up_w, L0_ffn_down_w, L0_ffn_shared_up, L0_ffn_shared_down):

    def _L0_attn_ref(x, ln_w, ln_b, proj_W, proj_b, fconv_W, fconv_b, bconv_W, bconv_b, deltaBC_W, dt_W, dt_b, A_log, D):
        import jax, jax.numpy as jnp
        import numpy as np
        DIM = 256
        DT_RANK = 64
        D_STATE = 16
        BATCH = 2
        SEQ = 512
        EPS = 1e-05

        def _selective_scan(u, delta, A, B, C, D):
            deltaA = jnp.exp(jnp.einsum('bld,dn->bldn', delta, A))
            deltaBu = jnp.einsum('bld,bln->bldn', delta * u, B)

            def step(h, inp):
                dA, dBu, Ct = inp
                h = dA * h + dBu
                y = jnp.einsum('bdn,bn->bd', h, Ct)
                return (h, y)
            h0 = jnp.zeros((u.shape[0], u.shape[2], A.shape[1]), u.dtype)
            xs = (jnp.moveaxis(deltaA, 1, 0), jnp.moveaxis(deltaBu, 1, 0), jnp.moveaxis(C, 1, 0))
            _, ys = jax.lax.scan(step, h0, xs)
            y = jnp.moveaxis(ys, 0, 1)
            return y + u * D

        def _ssm(u, deltaBC_W, dt_W, dt_b, A_log, D):
            A = -jnp.exp(A_log)
            dbc = u @ deltaBC_W.T
            delta = dbc[..., :DT_RANK]
            B = dbc[..., DT_RANK:DT_RANK + D_STATE]
            C = dbc[..., DT_RANK + D_STATE:]
            delta = jax.nn.softplus(delta @ dt_W.T + dt_b)
            return _selective_scan(u, delta, A, B, C, D)
        skip = x
        mu = jnp.mean(x, axis=-1, keepdims=True)
        var = jnp.var(x, axis=-1, keepdims=True)
        xn = (x - mu) * jax.lax.rsqrt(var + EPS) * ln_w + ln_b
        xp = xn @ proj_W.T + proj_b

        def branch(W, b):
            u = jax.nn.softplus(xp @ W.T + b)
            return _ssm(u, deltaBC_W, dt_W, dt_b, A_log, D)
        x1 = branch(fconv_W, fconv_b)
        x2 = branch(bconv_W, bconv_b)
        z = xp * jax.nn.sigmoid(xp)
        return x1 * z + x2 * z + skip

    def _L0_ffn_ref(hidden_states, gate_w, bias_e, up_w, down_w, shared_up, shared_down):
        import jax, jax.numpy as jnp
        import numpy as np
        DIM = 256
        N_EXPERTS = 16
        TOP_K = 4
        N_GROUP = 4
        TOPK_GROUP = 2
        MOE_INTER = 128
        SHARED_INTER = 512
        ROUTED_SCALE = 2.5

        def relu2(x):
            return jnp.square(jax.nn.relu(x))

        def _router(x2, gate_w, bias_e):
            T = x2.shape[0]
            logits = x2 @ gate_w.T
            scores = jax.nn.sigmoid(logits)
            sc = jax.lax.stop_gradient(scores + bias_e[None, :])
            grp = sc.reshape(T, N_GROUP, N_EXPERTS // N_GROUP)
            top2, _ = jax.lax.top_k(grp, 2)
            group_scores = top2.sum(-1)
            _, gidx = jax.lax.top_k(group_scores, TOPK_GROUP)
            rows = jnp.arange(T)[:, None]
            gmask = jnp.zeros((T, N_GROUP), dtype=sc.dtype).at[rows, gidx].set(1.0)
            smask = jnp.repeat(gmask, N_EXPERTS // N_GROUP, axis=1)
            masked = jnp.where(smask > 0, sc, 0.0)
            _, topk_idx = jax.lax.top_k(masked, TOP_K)
            topk_w = jnp.take_along_axis(scores, topk_idx, axis=1)
            topk_w = topk_w / (topk_w.sum(-1, keepdims=True) + 1e-20)
            topk_w = topk_w * ROUTED_SCALE
            return (topk_idx, topk_w)
        B, S, D = hidden_states.shape
        x2 = hidden_states.reshape(-1, D)
        T = x2.shape[0]
        topk_idx, topk_w = _router(x2, gate_w, bias_e)
        rows = jnp.arange(T)[:, None]
        combine = jnp.zeros((T, N_EXPERTS), dtype=topk_w.dtype).at[rows, topk_idx].add(topk_w)

        def body(acc, inp):
            wu, wd, cw = inp
            y = relu2(x2 @ wu.T) @ wd.T
            return (acc + cw[:, None] * y, None)
        routed, _ = jax.lax.scan(body, jnp.zeros_like(x2), (up_w, down_w, combine.T))
        shared = relu2(x2 @ shared_up.T) @ shared_down.T
        out = routed + shared
        return out.reshape(B, S, D)
    x = L0_attn_x
    x = x + _L0_attn_ref(_layernorm(x, axis=-1), L0_attn_ln_w, L0_attn_ln_b, L0_attn_proj_W, L0_attn_proj_b, L0_attn_fconv_W, L0_attn_fconv_b, L0_attn_bconv_W, L0_attn_bconv_b, L0_attn_deltaBC_W, L0_attn_dt_W, L0_attn_dt_b, L0_attn_A_log, L0_attn_D)
    x = x + _L0_ffn_ref(_layernorm(x, axis=-1), L0_ffn_gate_w, L0_ffn_bias_e, L0_ffn_up_w, L0_ffn_down_w, L0_ffn_shared_up, L0_ffn_shared_down)
    return x

_drawn_inputs = setup_inputs


def setup_inputs(seed=0):
    import zlib

    import numpy as np

    out = dict(_drawn_inputs(seed))
    spreads = {'L0_attn_ln_w': (1.0, 0.6),
     'L0_attn_ln_b': (0.0, 0.8),
     'L0_attn_proj_b': (0.0, 0.275),
     'L0_attn_fconv_b': (0.0, 0.8),
     'L0_attn_bconv_b': (0.0, 0.8),
     'L0_attn_dt_b': (0.0, 0.8),
     'L0_attn_D': (1.0, 0.6),
     'L0_ffn_bias_e': (0.0, 2.0)}
    factors = {'L0_attn_fconv_W': 8.0,
     'L0_attn_bconv_W': 8.0,
     'L0_attn_deltaBC_W': 8.0,
     'L0_attn_dt_W': 8.0,
     'L0_attn_A_log': 8.0,
     'L0_ffn_gate_w': 33.008,
     'L0_ffn_up_w': 27.928,
     'L0_ffn_down_w': 25.568,
     'L0_ffn_shared_up': 8.0,
     'L0_ffn_shared_down': 8.0}
    for name, (base, spread) in spreads.items():
        noise = np.random.default_rng([zlib.crc32(name.encode()), seed]).standard_normal(out[name].shape)
        drawn = base * np.exp(spread * noise) if base else spread * noise
        out[name] = jnp.asarray(drawn.astype(out[name].dtype))
    for name, factor in factors.items():
        out[name] = (out[name] * factor).astype(out[name].dtype)
    return out
```

```python
import concourse.bass as bass
from concourse import mybir
from contextlib import ExitStack

BATCH, SEQ, DIM = 8, 512, 256
STATES, DT_RANK = 16, 64
EXPERTS, INTER, SHARED = 16, 128, 512
GROUPS, TOP_GROUPS, TOP_K, ROUTED_SCALE = 4, 2, 4, 2.5
EPS = 1e-5
P = 128
TT = SEQ // P
CT = DIM // P
BRANCHES = 2
UNITS = BRANCHES * CT
SLOTS = 2 * STATES
HALF = SEQ // 2
SHARED_PAIRS = SHARED // P // 2
EXPERT_PAIRS = EXPERTS // 2
PAIRS = SHARED_PAIRS + EXPERT_PAIRS
ROWS_B = DT_RANK + STATES
SOFTPLUS_CLAMP = 40.0

UP_SLOT = [5, 7] + list(range(10, 18)) + list(range(19, 29))
OUT_SLOT = [UP_SLOT[PAIRS - 1] + 3, UP_SLOT[2 * PAIRS - 1] + 3]
assert len(UP_SLOT) == 2 * PAIRS

STATE_RING, B_RING, CW_RING = 8, 4, 2


class Steps:

    def __init__(self, sem, names):
        self.sem, self.names, self.at = sem, names, 0

    def inc(self, name):
        assert self.names[self.at] == name, (name, self.names[self.at])
        self.at = (self.at + 1) % len(self.names)
        return self.sem, 1

    def by(self, b, name):
        return b * len(self.names) + (self.names.index(name) + 1)


def norm_steps(tag):
    return [f"{tag}_stats", f"{tag}_moments", f"{tag}_var", f"{tag}_y2", f"{tag}_vy2", f"{tag}_corr", f"{tag}_rstd"]


PREP_VECTOR = (norm_steps("outer") + ["xl", "xs"] + norm_steps("inner") + ["xn"]
               + ["z_den", "z_sig", "z"] + ["u_min", "u_max", "u"]
               + ["c_hi", "c_r1a", "c_r1b", "c_mid_a", "c_mid_b", "c_r2", "c_lo"]
               + ["d_min", "d_max", "delta"] + ["du"] + ["ud_0", "ud"])
PREP_SCALAR = ["outer_ln", "outer_y", "inner_ln", "inner_y", "xnT0", "xnT1", "xp0", "xp1",
               "u0", "u1", "z_exp", "u2", "u3", "zT0", "zT1", "u_exp", "u_ln", "db0", "db1", "c",
               "d0", "d1", "d2", "d3", "d_exp", "d_ln"]
PREP_TENSOR = ["xnT0", "xnT1", "xp0", "xp1", "u0", "u1", "u2", "u3", "zT0", "zT1", "db0", "db1", "c",
               "d0", "d1", "d2", "d3"]
PREP_POOL = ["u_lin", "u_low", "d_lin", "d_low"]

ROUTER_STEPS = 26
FFN_VECTOR = (["yz0", "yz1", "x1"] + norm_steps("ffn") + ["xf"] + [f"route{i}" for i in range(ROUTER_STEPS)])
FFN_TENSOR = ["xfT0", "xfT1", "logits"]
FFN_SCALAR = ["ffn_ln", "ffn_y", "xfT0", "xfT1", "z_logits"]
for _slot in range(SLOTS + 1):
    for _m, _up in enumerate(UP_SLOT):
        if _up == _slot:
            FFN_TENSOR.append(f"up{_m}")
            FFN_SCALAR += [f"relu{_m}", f"square{_m}"]
        if _up + 1 == _slot and _m % PAIRS >= SHARED_PAIRS:
            FFN_VECTOR.append(f"weigh{_m}")
        if _up + 2 == _slot:
            FFN_TENSOR.append(f"down{_m}")
    if _slot in OUT_SLOT:
        FFN_VECTOR.append(f"out{OUT_SLOT.index(_slot)}")
    if _slot == 7:
        FFN_TENSOR.append("cwT")
        FFN_SCALAR.append("cwT")


def block_kernel(nc, x, ln_w, ln_b, projT, proj_b, fT, f_b, bT, b_b, dbcT, dtT, dt_b, A_log, D,
                 gateT, bias_e, upT, downT, shared_upT, shared_downT, out):
    f32, bf16 = mybir.dt.float32, mybir.dt.bfloat16
    ALU = mybir.AluOpType
    ACT = mybir.ActivationFunctionType
    AX = mybir.AxisListType

    with ExitStack() as ctx:
        def sb(name, shape, dt=f32):
            return ctx.enter_context(nc.sbuf_tensor(name, shape, dt))

        def bank(name):
            return ctx.enter_context(nc.psum_tensor(name, [P, SEQ], f32))

        def sem(name):
            return ctx.enter_context(nc.semaphore(name))

        b_dram = nc.dram_tensor("b_rows", [BATCH, BRANCHES, STATES, SEQ], f32, kind="Internal").ap()
        cw_dram = nc.dram_tensor("cw_rows", [BATCH, EXPERTS, SEQ], f32, kind="Internal").ap()

        proj_sb = sb("proj_sb", [P, CT, DIM])
        branch_sb = sb("branch_sb", [P, BRANCHES, CT, DIM])
        dbc_sb = sb("dbc_sb", [P, CT, ROWS_B + STATES])
        c_w = sb("c_w", [P, BRANCHES, CT, 96])
        dt_sb = sb("dt_sb", [DT_RANK, DIM])
        gate_sb = sb("gate_sb", [P, CT, EXPERTS])
        up_sb = sb("up_sb", [P, CT, EXPERTS * INTER])
        down_sb = sb("down_sb", [P, EXPERTS, DIM])
        sup_sb = sb("sup_sb", [P, CT, SHARED])
        sdown_sb = sb("sdown_sb", [P, SHARED // P, DIM])
        lnw_c, lnb_c, projb_c, dtb_c, d_c = [sb(n, [P, CT]) for n in ("lnw_c", "lnb_c", "projb_c", "dtb_c", "d_c")]
        branchb_c = sb("branchb_c", [P, BRANCHES, CT])
        neg_a = sb("neg_a", [P, CT, STATES])
        bias_sb = sb("bias_sb", [P, EXPERTS])
        ident = sb("ident", [P, P])
        pick = sb("pick", [96, 32], bf16)
        lower = sb("lower", [P, GROUPS, GROUPS])
        restart = sb("restart", [P, TT * EXPERTS])

        x_sb = sb("x_sb", [P, TT, DIM])
        xnT = x_sb[:, :, :].rearrange("p a b -> p (a b)").rearrange("p (c t) -> p c t", c=CT)
        xl = sb("xl", [P, TT, DIM])
        z_sb = xl[:, :, :].rearrange("p a b -> p (a b)").rearrange("p (c t) -> p c t", c=CT)
        xs = sb("xs", [P, 2, TT, DIM])
        zT = sb("zT", [P, 2, TT, DIM])
        xpT = sb("xpT", [P, CT, SEQ])
        pre = sb("pre", [P, UNITS, SEQ])
        ex = sb("ex", [P, UNITS, SEQ])
        xn = ex[:, 0:2, :].rearrange("p a b -> p (a b)").rearrange("p (c t) -> p c t", c=TT)
        u_sb = sb("u_sb", [P, UNITS, SEQ])
        ud = sb("ud", [P, CT, SEQ])
        delta = sb("delta", [P, 2, UNITS, SEQ])
        du = sb("du", [P, 2, UNITS, SEQ])
        low = sb("low", [ROWS_B, BRANCHES, SEQ])
        c_sb = sb("c_sb", [96, SEQ])
        c_parts = sb("c_parts", [96, 2, SEQ], bf16)
        stats = sb("stats", [P, TT, 6])
        mv = sb("mv", [P, TT, 2])
        nv, ny, nt, nr = [sb(n, [P, TT]) for n in ("nv", "ny", "nt", "nr")]

        b_ring = sb("b_ring", [P, B_RING, BRANCHES, SEQ])
        state = sb("state", [P, STATE_RING, SEQ])

        x1 = sb("x1", [P, TT, DIM])
        act_sb = sb("act_sb", [P, 2, 2, HALF])
        xf = act_sb[:, :, :, :].rearrange("p a b c -> p a (b c)").rearrange("p a b -> p (a b)").rearrange(
            "p (c t) -> p c t", c=TT)
        xfT = sb("xfT", [P, CT, SEQ])
        hidden = sb("hidden", [P, 2, 2, HALF])
        cw_ring = sb("cw_ring", [P, CW_RING, 2, HALF])
        cwT = sb("cwT", [EXPERTS, SEQ])
        out_sb = sb("out_sb", [P, 2, DIM])
        fstats = sb("fstats", [P, TT, 6])
        fmv = sb("fmv", [P, TT, 2])
        fv, fy, ft, fr = [sb(n, [P, TT]) for n in ("fv", "fy", "ft", "fr")]
        TE = TT * EXPERTS
        r_e, r_s, r_b, r_m, r_g, r_q, r_w = [sb(n, [P, TE]) for n in ("r_e", "r_s", "r_b", "r_m", "r_g", "r_q", "r_w")]
        r_hi, r_lo = [sb(n, [P, TE // 2]) for n in ("r_hi", "r_lo")]
        r_t1, r_t2, r_gs, r_gk = [sb(n, [P, TT * GROUPS]) for n in ("r_t1", "r_t2", "r_gs", "r_gk")]
        r_c1, r_c2 = [sb(n, [P, TT, GROUPS, GROUPS]) for n in ("r_c1", "r_c2")]
        r_top = sb("r_top", [P, TT, 8])
        r_n, r_sum = [sb(n, [P, TT]) for n in ("r_n", "r_sum")]

        prep_bank, ffn_bank, down_bank, c_bank = bank("prep_bank"), bank("ffn_bank"), bank("down_bank"), bank("c_bank")
        decay = [bank("decay0"), bank("decay1")]
        y_bank = [bank("y0"), bank("y1")]

        weights_in = sem("weights_in")
        pool_consts = sem("pool_consts")
        vector_consts = sem("vector_consts")
        a_exp = sem("a_exp")
        x_in = sem("x_in")
        b_stored = sem("b_stored")
        b_in = [sem(f"b_in{i}") for i in range(B_RING)]
        cw_stored = sem("cw_stored")
        cw_in = [sem(f"cw_in{i}") for i in range(CW_RING)]
        out_stored = sem("out_stored")
        decay_done = sem("decay_done")
        input_done = sem("input_done")
        scan_done = sem("scan_done")
        yc_done = sem("yc_done")
        c_done = sem("c_done")
        y_started = sem("y_started")
        y_added = sem("y_added")
        pv = Steps(sem("prep_vector"), PREP_VECTOR)
        ps = Steps(sem("prep_scalar"), PREP_SCALAR)
        pt = Steps(sem("prep_tensor"), PREP_TENSOR)
        pp = Steps(sem("prep_pool"), PREP_POOL)
        fve = Steps(sem("ffn_vector"), FFN_VECTOR)
        fs = Steps(sem("ffn_scalar"), FFN_SCALAR)
        fte = Steps(sem("ffn_tensor"), FFN_TENSOR)

        block = ctx.enter_context(nc.Block())

        def run(engine, prep, scan, ffn):
            def slots(b, do_prep=True, do_scan=True, do_ffn=True):
                for s in range(SLOTS):
                    if do_scan:
                        scan(b, s)
                    if do_ffn:
                        ffn(b - 1, s)
                    if do_prep:
                        prep(b + 1, s)
            slots(-1, do_scan=False, do_ffn=False)
            for b in range(BATCH):
                slots(b, do_prep=b + 1 < BATCH, do_ffn=b > 0)
            slots(BATCH, do_prep=False, do_scan=False)

        WEIGHTS = 16 * (4 * CT + 2 * CT + 1 + 2 * CT + CT + 1 + 1 + 5 * 1 + 2 + 1 + 1)
        loads = []

        @block.sync
        def _(sp):
            def load(dst, src):
                loads.append(1)
                sp.dma_start(dst, src).then_inc(weights_in, 16)

            def load_x(b):
                if b > 0:
                    sp.wait_ge(pt.sem, pt.by(b - 1, "xp1"))
                sp.dma_start(x_sb[:, :, :], x[b, :, :].rearrange("(t p) c -> p t c", p=P)).then_inc(x_in, 16)

            load_x(0)
            with nc.allow_non_contiguous_dma(reason="a few columns of constants"):
                load(lnw_c[:, :], ln_w.rearrange("(c p) -> p c", p=P))
                load(lnb_c[:, :], ln_b.rearrange("(c p) -> p c", p=P))
                load(projb_c[:, :], proj_b.rearrange("(c p) -> p c", p=P))
                load(branchb_c[:, 0, :], f_b.rearrange("(c p) -> p c", p=P))
                load(branchb_c[:, 1, :], b_b.rearrange("(c p) -> p c", p=P))
                load(dtb_c[:, :], dt_b.rearrange("(c p) -> p c", p=P))
                load(d_c[:, :], D.rearrange("(c p) -> p c", p=P))
            load(neg_a[:, :, :], A_log.rearrange("(c p) n -> p c n", p=P))
            load(proj_sb[:, :, :], projT.rearrange("(c p) n -> p c n", p=P))
            load(branch_sb[:, 0, :, :], fT.rearrange("(c p) n -> p c n", p=P))
            load(branch_sb[:, 1, :, :], bT.rearrange("(c p) n -> p c n", p=P))
            load(dbc_sb[:, :, :], dbcT.rearrange("(c p) n -> p c n", p=P))
            load(dt_sb[:, :], dtT)
            load(gate_sb[:, :, :], gateT.rearrange("(c p) n -> p c n", p=P))
            load(bias_sb[:, :], bias_e.rearrange("(a n) -> a n", a=1).partition_broadcast(P) if False else
                 bias_e.partition_broadcast(P))
            load(sup_sb[:, :, :], shared_upT.rearrange("(c p) n -> p c n", p=P))
            load(sdown_sb[:, :, :], shared_downT.rearrange("(c p) n -> p c n", p=P))
            load(up_sb[:, :, :], upT.rearrange("(c p) n -> p c n", p=P))
            load(down_sb[:, :, :], downT.rearrange("e p n -> p e n"))

            def load_b(b, n):
                step = b * STATES + n
                if step >= B_RING:
                    sp.wait_ge(input_done, UNITS * (step - B_RING + 1))
                sp.wait_ge(b_stored, 16 * BRANCHES * (b + 1))
                sp.dma_start(b_ring[:, n % B_RING, :, :],
                             b_dram[b, :, n, :].partition_broadcast(P)).then_inc(b_in[n % B_RING], 16)

            def prep(b, s):
                if s == 15:
                    for r in range(BRANCHES):
                        sp.wait_ge(ps.sem, ps.by(b, f"db{r}"))
                        sp.dma_start(b_dram[b, r, :, :], low[DT_RANK:ROWS_B, r, :]).then_inc(b_stored, 16)
                if s == 20 and b + 1 < BATCH:
                    load_x(b + 1)
                if b == 0 and s == SLOTS - 1:
                    for n in range(B_RING - 1):
                        load_b(0, n)

            def scan(b, s):
                if s % 2 == 0:
                    n = s // 2 + B_RING - 1
                    if n < STATES:
                        load_b(b, n)
                    elif b + 1 < BATCH:
                        load_b(b + 1, n - STATES)

            def ffn(b, s):
                if s == 7:
                    sp.wait_ge(fs.sem, fs.by(b, "cwT"))
                    sp.dma_start(cw_dram[b, :, :], cwT[:, :]).then_inc(cw_stored, 16)
                for m, up in enumerate(UP_SLOT):
                    k = m % PAIRS - SHARED_PAIRS
                    if k >= 0 and up - 1 == s:
                        e, half, slot = 2 * k, m // PAIRS, m % CW_RING
                        before = m - CW_RING if k >= CW_RING else m - CW_RING - SHARED_PAIRS
                        if before > 0:
                            sp.wait_ge(fve.sem, fve.by(b, f"weigh{before}"))
                        elif b > 0:
                            sp.wait_ge(fve.sem, fve.by(b - 1, f"weigh{before + 2 * PAIRS}"))
                        sp.wait_ge(cw_stored, 16 * (b + 1))
                        sp.dma_start(cw_ring[:, slot, :, :],
                                     cw_dram[b, e:e + 2, half * HALF:(half + 1) * HALF].partition_broadcast(P)
                                     ).then_inc(cw_in[slot], 16)
                for half in range(2):
                    if OUT_SLOT[half] == s:
                        sp.wait_ge(fve.sem, fve.by(b, f"out{half}"))
                        sp.dma_start(out[b, half * HALF:(half + 1) * HALF, :].rearrange("(t p) c -> p t c", p=P),
                                     out_sb[:, :, :]).then_inc(out_stored, 16)

            run(sp, prep, scan, ffn)
            sp.wait_ge(out_stored, 16 * 2 * BATCH)

        WEIGHTS = 16 * len(loads)

        @block.gpsimd
        def _(pool):
            nc.gpsimd.memset(ident[:, :], 0.0).then_inc(pool_consts, 1)
            nc.gpsimd.memset(pick[:, :], 0.0).then_inc(pool_consts, 1)
            nc.gpsimd.memset(lower[:, :, :], 1.0).then_inc(pool_consts, 1)
            pool.wait_ge(pool_consts, 3)
            nc.gpsimd.affine_select(out=ident[:, :], in_=ident[:, :], compare_op=ALU.not_equal, fill=1.0,
                                    base=0, pattern=[[-1, P]], channel_multiplier=1).then_inc(pool_consts, 1)
            nc.gpsimd.affine_select(out=lower[:, :, :], in_=lower[:, :, :], compare_op=ALU.is_gt, fill=0.0,
                                    base=0, pattern=[[1, GROUPS], [-1, GROUPS]], channel_multiplier=0
                                    ).then_inc(pool_consts, 1)
            for part in range(3):
                pool.wait_ge(pool_consts, 5 + part)
                nc.gpsimd.affine_select(out=pick[:, :], in_=pick[:, :], compare_op=ALU.not_equal, fill=1.0,
                                        base=-32 * part, pattern=[[-1, 32]], channel_multiplier=1
                                        ).then_inc(pool_consts, 1)

            def lower_bound(b, tag, dst):
                pool.wait_ge(ps.sem, ps.by(b, f"{tag}_exp"))
                nc.gpsimd.tensor_scalar(dst, ex[:, :, :], -0.5, 1.0, ALU.mult, ALU.add
                                        ).then_inc(*pp.inc(f"{tag}_lin"))
                pool.wait_ge(pp.sem, pp.by(b, f"{tag}_lin"))
                nc.gpsimd.tensor_tensor(dst, dst, ex[:, :, :], ALU.mult).then_inc(*pp.inc(f"{tag}_low"))

            def prep(b, s):
                if s == 10:
                    if b > 0:
                        pool.wait_ge(pv.sem, pv.by(b - 1, "ud"))
                        pool.wait_ge(pt.sem, pt.by(b - 1, "c"))
                    lower_bound(b, "u", u_sb[:, :, :])
                if s == 19:
                    if b > 1:
                        pool.wait_ge(decay_done, UNITS * STATES * (b - 1))
                        pool.wait_ge(pv.sem, pv.by(b - 2, "du"))
                    lower_bound(b, "d", delta[:, b % 2, :, :])

            def scan(b, s):
                n = s // 2
                for j in (2 * (s % 2), 2 * (s % 2) + 1):
                    g = n * UNITS + j
                    r = j // CT
                    if g == 0:
                        pool.wait_ge(pv.sem, pv.by(b, "du"))
                    if j == 0:
                        step = b * STATES + n
                        pool.wait_ge(b_in[n % B_RING], 16 * (step // B_RING + 1))
                    if b * STATES * UNITS + g >= STATE_RING:
                        pool.wait_ge(y_added, b * STATES * UNITS + g - STATE_RING + 1)
                    nc.gpsimd.tensor_tensor(state[:, g % STATE_RING, :], du[:, b % 2, j, :],
                                            b_ring[:, n % B_RING, r, :], ALU.mult).then_inc(input_done, 1)

            run(pool, prep, scan, lambda b, s: None)

        @block.scalar
        def _(act):
            act.wait_ge(weights_in, WEIGHTS)
            nc.scalar.activation(neg_a[:, :, :], neg_a[:, :, :], ACT.Exp).then_inc(a_exp, 1)

            def rsqrt_guess(b, steps, vsteps, tag, v, y):
                act.wait_ge(vsteps.sem, vsteps.by(b, f"{tag}_var"))
                nc.scalar.activation(y[:, :], v[:, :], ACT.Ln).then_inc(*steps.inc(f"{tag}_ln"))
                act.wait_ge(steps.sem, steps.by(b, f"{tag}_ln"))
                nc.scalar.activation(y[:, :], y[:, :], ACT.Exp, scale=-0.5).then_inc(*steps.inc(f"{tag}_y"))

            def evacuate(b, name, dst, bias=0.0, scale=1.0, src=None):
                act.wait_ge(pt.sem, pt.by(b, name))
                nc.scalar.activation(dst, prep_bank[:, :] if src is None else src, ACT.Identity, bias=bias,
                                     scale=scale).then_inc(*ps.inc(name))

            def softplus_exp(b, tag):
                act.wait_ge(pv.sem, pv.by(b, f"{tag}_min"))
                nc.scalar.activation(ex[:, :, :], ex[:, :, :], ACT.Exp).then_inc(*ps.inc(f"{tag}_exp"))

            def softplus_ln(b, tag):
                act.wait_ge(pp.sem, pp.by(b, f"{tag}_low"))
                nc.scalar.activation(ex[:, :, :], ex[:, :, :], ACT.Ln, bias=1.0).then_inc(*ps.inc(f"{tag}_ln"))

            def prep(b, s):
                if s == 1:
                    rsqrt_guess(b, ps, pv, "outer", nv, ny)
                if s == 3:
                    rsqrt_guess(b, ps, pv, "inner", nv, ny)
                if s == 5:
                    for c in range(CT):
                        evacuate(b, f"xnT{c}", xnT[:, c, :], lnb_c[:, c:c + 1], lnw_c[:, c:c + 1])
                if s == 6:
                    for c in range(CT):
                        evacuate(b, f"xp{c}", xpT[:, c, :], projb_c[:, c:c + 1])
                if s in (7, 8):
                    r = s - 7
                    if r == 0 and b > 0:
                        act.wait_ge(pv.sem, pv.by(b - 1, "delta"))
                    for c in range(CT):
                        evacuate(b, f"u{r * CT + c}", pre[:, r * CT + c, :], branchb_c[:, r, c:c + 1])
                    if r == 0:
                        act.wait_ge(pv.sem, pv.by(b, "xn"))
                        nc.scalar.activation(z_sb, xpT[:, :, :], ACT.Exp, scale=-1.0).then_inc(*ps.inc("z_exp"))
                if s == 9:
                    if b > 1:
                        act.wait_ge(fve.sem, fve.by(b - 2, "yz1"))
                    for c in range(CT):
                        evacuate(b, f"zT{c}", zT[:, b % 2, :, c * P:(c + 1) * P], src=prep_bank[:, :].rearrange("p (t c) -> p t c", t=TT))
                if s == 10:
                    softplus_exp(b, "u")
                if s == 12:
                    softplus_ln(b, "u")
                if s == 14:
                    for r in range(BRANCHES):
                        if b > 0 and r == 0:
                            act.wait_ge(b_stored, 16 * BRANCHES * b)
                            act.wait_ge(pt.sem, pt.by(b - 1, "d3"))
                        evacuate(b, f"db{r}", low[:, r, :], src=prep_bank[0:ROWS_B, :])
                if s == 15:
                    evacuate(b, "c", c_sb[:, :], src=prep_bank[0:96, :])
                if s in (16, 17):
                    if s == 16:
                        act.wait_ge(pv.sem, pv.by(b, "u"))
                    for j in (2 * (s - 16), 2 * (s - 16) + 1):
                        c = j % CT
                        evacuate(b, f"d{j}", pre[:, j, :], dtb_c[:, c:c + 1])
                if s == 19:
                    softplus_exp(b, "d")
                if s == 21:
                    softplus_ln(b, "d")

            def scan(b, s):
                n = s // 2
                for j in (2 * (s % 2), 2 * (s % 2) + 1):
                    g = n * UNITS + j
                    total = b * STATES * UNITS + g
                    if g == 0:
                        act.wait_ge(pv.sem, pv.by(b, "delta"))
                        if b == 0:
                            act.wait_ge(vector_consts, 2)
                    if total >= 2:
                        act.wait_ge(scan_done, total - 1)
                    nc.scalar.activation(decay[g % 2][:, :], delta[:, b % 2, j, :], ACT.Exp,
                                         scale=neg_a[:, j % CT, n:n + 1]).then_inc(decay_done, 1)

            def ffn(b, s):
                if s == 1:
                    rsqrt_guess(b, fs, fve, "ffn", fv, fy)
                if s == 3:
                    for c in range(CT):
                        act.wait_ge(fte.sem, fte.by(b, f"xfT{c}"))
                        if b > 0 and c == 0:
                            act.wait_ge(fte.sem, fte.by(b - 1, f"up{2 * PAIRS - 1}"))
                        nc.scalar.activation(xfT[:, c, :], ffn_bank[:, :], ACT.Identity).then_inc(*fs.inc(f"xfT{c}"))
                if s == 4:
                    act.wait_ge(fte.sem, fte.by(b, "logits"))
                    nc.scalar.activation(r_e[:, :], ffn_bank[:, 0:TE], ACT.Exp, scale=-1.0).then_inc(*fs.inc("z_logits"))
                for m, up in enumerate(UP_SLOT):
                    if up == s:
                        shared = m % PAIRS < SHARED_PAIRS
                        if m >= 2 and (m - 2) % PAIRS >= SHARED_PAIRS:
                            act.wait_ge(fve.sem, fve.by(b, f"weigh{m - 2}"))
                        elif m < 2 and b > 0:
                            act.wait_ge(fve.sem, fve.by(b - 1, f"weigh{2 * PAIRS - 2 + m}"))
                        act.wait_ge(fte.sem, fte.by(b, f"up{m}"))
                        a = act_sb[:, m % 2, :, :].rearrange("p a b -> p (a b)")
                        nc.scalar.activation(a, ffn_bank[:, :], ACT.Relu).then_inc(*fs.inc(f"relu{m}"))
                        if shared:
                            if m >= 2:
                                act.wait_ge(fte.sem, fte.by(b, f"down{m - 2}"))
                            elif b > 0:
                                act.wait_ge(fte.sem, fte.by(b - 1, f"down{2 * PAIRS - 2 + m}"))
                        act.wait_ge(fs.sem, fs.by(b, f"relu{m}"))
                        dst = hidden[:, m % 2, :, :].rearrange("p a b -> p (a b)") if shared else a
                        nc.scalar.activation(dst, a, ACT.Square).then_inc(*fs.inc(f"square{m}"))
                if s == 7:
                    act.wait_ge(fte.sem, fte.by(b, "cwT"))
                    if b > 0:
                        act.wait_ge(cw_stored, 16 * b)
                    nc.scalar.activation(cwT[:, :], ffn_bank[0:EXPERTS, :], ACT.Identity).then_inc(*fs.inc("cwT"))

            run(act, prep, scan, ffn)

        @block.vector
        def _(dve):
            dve.wait_ge(weights_in, WEIGHTS)
            dve.wait_ge(a_exp, 1)
            nc.vector.tensor_scalar(neg_a[:, :, :], neg_a[:, :, :], -1.0, None, ALU.mult).then_inc(vector_consts, 1)
            nc.vector.memset(c_w[:, :, :, :], 0.0).then_inc(vector_consts, 1)
            nc.vector.memset(restart[:, :], 1.0).then_inc(vector_consts, 1)
            dve.wait_ge(vector_consts, 3)
            nc.vector.memset(restart[:, :].rearrange("p (t e) -> p t e", e=EXPERTS)[:, :, 0:1], 0.0
                             ).then_inc(vector_consts, 1)
            for r in range(BRANCHES):
                for part in range(3):
                    col = 32 * part + STATES * r
                    nc.vector.tensor_copy(c_w[:, r, :, col:col + STATES], dbc_sb[:, :, ROWS_B:ROWS_B + STATES]
                                          ).then_inc(vector_consts, 1)
            dve.wait_ge(pool_consts, 8)
            dve.wait_ge(vector_consts, 4 + 3 * BRANCHES)

            def norm_moments(b, steps, tag, src, st, m, v):
                for t in range(TT):
                    last = nc.vector.bn_stats(st[:, t, :], src[:, t, :])
                last.then_inc(*steps.inc(f"{tag}_stats"))
                dve.wait_ge(steps.sem, steps.by(b, f"{tag}_stats"))
                for t in range(TT):
                    last = nc.vector.bn_aggr(m[:, t, :], st[:, t, :])
                last.then_inc(*steps.inc(f"{tag}_moments"))
                dve.wait_ge(steps.sem, steps.by(b, f"{tag}_moments"))
                nc.vector.tensor_scalar(v[:, :], m[:, :, 1], EPS, None, ALU.add).then_inc(*steps.inc(f"{tag}_var"))

            def norm_apply(b, steps, ssteps, tag, dst, src, m, v, y, t_, r_, done):
                dve.wait_ge(ssteps.sem, ssteps.by(b, f"{tag}_y"))
                nc.vector.tensor_tensor(t_[:, :], y[:, :], y[:, :], ALU.mult).then_inc(*steps.inc(f"{tag}_y2"))
                dve.wait_ge(steps.sem, steps.by(b, f"{tag}_y2"))
                nc.vector.tensor_tensor(t_[:, :], t_[:, :], v[:, :], ALU.mult).then_inc(*steps.inc(f"{tag}_vy2"))
                dve.wait_ge(steps.sem, steps.by(b, f"{tag}_vy2"))
                nc.vector.tensor_scalar(t_[:, :], t_[:, :], -0.5, 1.5, ALU.mult, ALU.add
                                        ).then_inc(*steps.inc(f"{tag}_corr"))
                dve.wait_ge(steps.sem, steps.by(b, f"{tag}_corr"))
                nc.vector.tensor_tensor(r_[:, :], y[:, :], t_[:, :], ALU.mult).then_inc(*steps.inc(f"{tag}_rstd"))
                dve.wait_ge(steps.sem, steps.by(b, f"{tag}_rstd"))
                for t in range(TT):
                    last = nc.vector.tensor_scalar(dst[:, t, :], src[:, t, :], m[:, t, 0:1], r_[:, t:t + 1],
                                                   ALU.subtract, ALU.mult)
                last.then_inc(*steps.inc(done))

            def softplus_min(b, tag):
                dve.wait_ge(ps.sem, ps.by(b, f"{tag}3"))
                nc.vector.tensor_scalar(ex[:, :, :], pre[:, :, :], SOFTPLUS_CLAMP, None, ALU.min
                                        ).then_inc(*pv.inc(f"{tag}_min"))

            def softplus_max(b, tag, dst, done):
                dve.wait_ge(ps.sem, ps.by(b, f"{tag}_ln"))
                nc.vector.tensor_tensor(pre[:, :, :], pre[:, :, :], ex[:, :, :], ALU.max).then_inc(*pv.inc(f"{tag}_max"))
                dve.wait_ge(pv.sem, pv.by(b, f"{tag}_max"))
                nc.vector.tensor_tensor(dst, dst, pre[:, :, :], ALU.max).then_inc(*pv.inc(done))

            def prep(b, s):
                if s == 0:
                    dve.wait_ge(x_in, 16 * (b + 1))
                    norm_moments(b, pv, "outer", x_sb, stats, mv, nv)
                if s == 2:
                    if b > 0:
                        dve.wait_ge(pt.sem, pt.by(b - 1, "zT1"))
                    norm_apply(b, pv, ps, "outer", xl, x_sb, mv, nv, ny, nt, nr, "xl")
                    dve.wait_ge(pv.sem, pv.by(b, "xl"))
                    nc.vector.tensor_tensor(xs[:, b % 2, :, :], x_sb[:, :, :], xl[:, :, :], ALU.add
                                            ).then_inc(*pv.inc("xs"))
                    norm_moments(b, pv, "inner", xl, stats, mv, nv)
                if s == 4:
                    norm_apply(b, pv, ps, "inner", xn, xl, mv, nv, ny, nt, nr, "xn")
                if s == 8:
                    dve.wait_ge(ps.sem, ps.by(b, "z_exp"))
                    nc.vector.tensor_scalar(z_sb, z_sb, 1.0, None, ALU.add).then_inc(*pv.inc("z_den"))
                    dve.wait_ge(pv.sem, pv.by(b, "z_den"))
                    nc.vector.reciprocal(z_sb, z_sb).then_inc(*pv.inc("z_sig"))
                    dve.wait_ge(pv.sem, pv.by(b, "z_sig"))
                    nc.vector.tensor_tensor(z_sb, z_sb, xpT[:, :, :], ALU.mult).then_inc(*pv.inc("z"))
                if s == 9:
                    dve.wait_ge(pt.sem, pt.by(b, "xnT1"))
                    softplus_min(b, "u")
                if s == 13:
                    softplus_max(b, "u", u_sb[:, :, :], "u")
                if s == 17:
                    dve.wait_ge(ps.sem, ps.by(b, "c"))
                    part = c_parts[:, b % 2, :]
                    nc.vector.tensor_copy(part, c_sb[:, :]).then_inc(*pv.inc("c_hi"))
                    dve.wait_ge(pv.sem, pv.by(b, "c_hi"))
                    for rows, name in ((slice(32, 64), "c_r1a"), (slice(64, 96), "c_r1b")):
                        nc.vector.tensor_tensor(c_sb[rows, :], c_sb[rows, :], c_parts[rows, b % 2, :], ALU.subtract
                                                ).then_inc(*pv.inc(name))
                    dve.wait_ge(pv.sem, pv.by(b, "c_r1b"))
                    for rows, name in ((slice(32, 64), "c_mid_a"), (slice(64, 96), "c_mid_b")):
                        nc.vector.tensor_copy(c_parts[rows, b % 2, :], c_sb[rows, :]).then_inc(*pv.inc(name))
                    dve.wait_ge(pv.sem, pv.by(b, "c_mid_b"))
                    nc.vector.tensor_tensor(c_sb[64:96, :], c_sb[64:96, :], c_parts[64:96, b % 2, :], ALU.subtract
                                            ).then_inc(*pv.inc("c_r2"))
                    dve.wait_ge(pv.sem, pv.by(b, "c_r2"))
                    nc.vector.tensor_copy(c_parts[64:96, b % 2, :], c_sb[64:96, :]).then_inc(*pv.inc("c_lo"))
                if s == 18:
                    softplus_min(b, "d")
                if s == 22:
                    softplus_max(b, "d", delta[:, b % 2, :, :], "delta")
                if s == 23:
                    dve.wait_ge(pv.sem, pv.by(b, "delta"))
                    if b > 1:
                        dve.wait_ge(input_done, UNITS * STATES * (b - 1))
                    nc.vector.tensor_tensor(du[:, b % 2, :, :], delta[:, b % 2, :, :], u_sb[:, :, :], ALU.mult
                                            ).then_inc(*pv.inc("du"))
                if s == 24:
                    if b > 0:
                        dve.wait_ge(y_started, b)
                    for c in range(CT):
                        last = nc.vector.tensor_scalar(ud[:, c, :], u_sb[:, c, :], d_c[:, c:c + 1], None, ALU.mult)
                    last.then_inc(*pv.inc("ud_0"))
                    dve.wait_ge(pv.sem, pv.by(b, "ud_0"))
                    for c in range(CT):
                        last = nc.vector.scalar_tensor_tensor(ud[:, c, :], u_sb[:, CT + c, :], d_c[:, c:c + 1],
                                                              ud[:, c, :], ALU.mult, ALU.add)
                    last.then_inc(*pv.inc("ud"))

            def scan(b, s):
                n = s // 2
                pair = (2 * (s % 2), 2 * (s % 2) + 1)
                for j in pair:
                    g = n * UNITS + j
                    total = b * STATES * UNITS + g
                    dve.wait_ge(decay_done, total + 1)
                    dve.wait_ge(input_done, total + 1)
                    slot = state[:, g % STATE_RING, :]
                    nc.vector.tensor_tensor_scan(slot, decay[g % 2][:, :], slot, 0.0, ALU.mult, ALU.add
                                                 ).then_inc(scan_done, 1)
                for j in pair:
                    g = n * UNITS + j
                    total = b * STATES * UNITS + g
                    if j % CT == 0:
                        dve.wait_ge(c_done, b * STATES * BRANCHES + n * BRANCHES + j // CT + 1)
                    dve.wait_ge(scan_done, total + 1)
                    slot = state[:, g % STATE_RING, :]
                    nc.vector.tensor_tensor(slot, slot, c_bank[:, :], ALU.mult).then_inc(yc_done, 1)

            def route(b):
                at = [0]

                def link(ins):
                    ins.then_inc(*fve.inc(f"route{at[0]}"))
                    dve.wait_ge(fve.sem, fve.by(b, f"route{at[0]}"))
                    at[0] += 1

                def te(tile):
                    return tile[:, :].rearrange("p (t e) -> p t e", e=EXPERTS)

                tt_ = nc.vector.tensor_tensor
                dve.wait_ge(fs.sem, fs.by(b, "z_logits"))
                link(nc.vector.tensor_scalar(r_e[:, :], r_e[:, :], 1.0, None, ALU.add))
                link(nc.vector.reciprocal(r_s[:, :], r_e[:, :]))
                link(tt_(te(r_b), te(r_s), bias_sb[:, :].unsqueeze(1).to_broadcast([P, TT, EXPERTS]), ALU.add))
                two = r_b[:, :].rearrange("p (a b) -> p a b", b=2)
                tt_(r_hi[:, :], two[:, :, 0], two[:, :, 1], ALU.max)
                link(tt_(r_lo[:, :], two[:, :, 0], two[:, :, 1], ALU.min))
                hi = r_hi[:, :].rearrange("p (a b) -> p a b", b=2)
                lo = r_lo[:, :].rearrange("p (a b) -> p a b", b=2)
                tt_(r_gs[:, :], hi[:, :, 0], hi[:, :, 1], ALU.max)
                tt_(r_t1[:, :], hi[:, :, 0], hi[:, :, 1], ALU.min)
                link(tt_(r_t2[:, :], lo[:, :, 0], lo[:, :, 1], ALU.max))
                link(tt_(r_t1[:, :], r_t1[:, :], r_t2[:, :], ALU.max))
                link(tt_(r_gs[:, :], r_gs[:, :], r_t1[:, :], ALU.add))
                gs = r_gs[:, :].rearrange("p (t g) -> p t g", g=GROUPS)
                shape = [P, TT, GROUPS, GROUPS]
                own, other = gs.unsqueeze(3).to_broadcast(shape), gs.unsqueeze(2).to_broadcast(shape)
                tt_(r_c1[:, :, :, :], other, own, ALU.is_gt)
                link(tt_(r_c2[:, :, :, :], other, own, ALU.is_equal))
                link(tt_(r_c2[:, :, :, :], r_c2[:, :, :, :], lower[:, :, :].unsqueeze(1).to_broadcast(shape), ALU.mult))
                link(tt_(r_c1[:, :, :, :], r_c1[:, :, :, :], r_c2[:, :, :, :], ALU.add))
                link(nc.vector.tensor_reduce(r_gk[:, :], r_c1[:, :, :, :].rearrange("p t g h -> p (t g) h"), AX.X, ALU.add))
                link(nc.vector.tensor_scalar(r_gk[:, :], r_gk[:, :], float(TOP_GROUPS), None, ALU.is_lt))
                per = EXPERTS // GROUPS
                link(tt_(r_m[:, :].rearrange("p (g k) -> p g k", k=per), r_b[:, :].rearrange("p (g k) -> p g k", k=per),
                         r_gk[:, :].unsqueeze(2).to_broadcast([P, TT * GROUPS, per]), ALU.mult))
                for t in range(TT):
                    last = nc.vector.max(r_top[:, t, :], te(r_m)[:, t, :])
                link(last)
                fourth = r_top[:, :, TOP_K - 1:TOP_K].to_broadcast([P, TT, EXPERTS])
                tt_(te(r_g), te(r_m), fourth, ALU.is_gt)
                link(tt_(te(r_q), te(r_m), fourth, ALU.is_equal))
                link(nc.vector.tensor_reduce(r_n[:, :], te(r_g), AX.X, ALU.add))
                link(nc.vector.tensor_scalar(r_n[:, :], r_n[:, :], -1.0, float(TOP_K), ALU.mult, ALU.add))
                link(nc.vector.tensor_tensor_scan(r_m[:, :], restart[:, :], r_q[:, :], 0.0, ALU.mult, ALU.add))
                link(tt_(te(r_m), te(r_m), r_n[:, :].unsqueeze(2).to_broadcast([P, TT, EXPERTS]), ALU.is_le))
                link(tt_(r_q[:, :], r_q[:, :], r_m[:, :], ALU.mult))
                link(tt_(r_g[:, :], r_g[:, :], r_q[:, :], ALU.add))
                link(tt_(r_w[:, :], r_s[:, :], r_g[:, :], ALU.mult))
                link(nc.vector.tensor_reduce(r_sum[:, :], te(r_w), AX.X, ALU.add))
                link(nc.vector.tensor_scalar(r_sum[:, :], r_sum[:, :], 1e-20, None, ALU.add))
                link(nc.vector.reciprocal(r_sum[:, :], r_sum[:, :]))
                link(nc.vector.scalar_tensor_tensor(te(r_w), te(r_w), ROUTED_SCALE,
                                                    r_sum[:, :].unsqueeze(2).to_broadcast([P, TT, EXPERTS]),
                                                    ALU.mult, ALU.mult))
                assert at[0] == ROUTER_STEPS, at

            def ffn(b, s):
                if s == 0:
                    dve.wait_ge(y_added, UNITS * STATES * (b + 1))
                    if b > 0:
                        dve.wait_ge(fve.sem, fve.by(b - 1, "out1"))
                    for h in range(2):
                        nc.vector.tensor_tensor(x1[:, 2 * h:2 * h + 2, :], zT[:, b % 2, 2 * h:2 * h + 2, :],
                                                y_bank[h][:, :].rearrange("p (t c) -> p t c", t=2), ALU.mult
                                                ).then_inc(*fve.inc(f"yz{h}"))
                    dve.wait_ge(fve.sem, fve.by(b, "yz1"))
                    nc.vector.tensor_tensor(x1[:, :, :], x1[:, :, :], xs[:, b % 2, :, :], ALU.add
                                            ).then_inc(*fve.inc("x1"))
                    dve.wait_ge(fve.sem, fve.by(b, "x1"))
                    norm_moments(b, fve, "ffn", x1, fstats, fmv, fv)
                if s == 2:
                    norm_apply(b, fve, fs, "ffn", xf, x1, fmv, fv, fy, ft, fr, "xf")
                if s == 5:
                    route(b)
                for m, up in enumerate(UP_SLOT):
                    if up + 1 == s and m % PAIRS >= SHARED_PAIRS:
                        if m >= 2:
                            dve.wait_ge(fte.sem, fte.by(b, f"down{m - 2}"))
                        k = m % PAIRS - SHARED_PAIRS
                        uses = (m // PAIRS) * (EXPERT_PAIRS // CW_RING) + k // CW_RING + 1
                        dve.wait_ge(cw_in[m % CW_RING], 16 * (b * (2 * EXPERT_PAIRS // CW_RING) + uses))
                        dve.wait_ge(fs.sem, fs.by(b, f"square{m}"))
                        nc.vector.tensor_tensor(hidden[:, m % 2, :, :], act_sb[:, m % 2, :, :],
                                                cw_ring[:, m % CW_RING, :, :], ALU.mult).then_inc(*fve.inc(f"weigh{m}"))
                for half in range(2):
                    if OUT_SLOT[half] == s:
                        dve.wait_ge(fte.sem, fte.by(b, f"down{(half + 1) * PAIRS - 1}"))
                        if b > 0 or half > 0:
                            dve.wait_ge(out_stored, 16 * (2 * b + half))
                        nc.vector.tensor_tensor(out_sb[:, :, :], x1[:, 2 * half:2 * half + 2, :],
                                                down_bank[:, :].rearrange("p (t c) -> p t c", t=2), ALU.add
                                                ).then_inc(*fve.inc(f"out{half}"))

            run(dve, prep, scan, ffn)

        @block.tensor
        def _(pe):
            pe.wait_ge(weights_in, WEIGHTS)
            pe.wait_ge(pool_consts, 8)
            pe.wait_ge(vector_consts, 4 + 3 * BRANCHES)

            def prep_free(b, before):
                if before is not None:
                    pe.wait_ge(ps.sem, ps.by(b, before))
                elif b > 0:
                    pe.wait_ge(ps.sem, ps.by(b - 1, "d3"))

            def transposes(bank_, src, name, steps):
                for t in range(TT):
                    last = nc.tensor.transpose(bank_[:, t * P:(t + 1) * P], src(t), ident[:, :])
                last.then_inc(*steps.inc(name))

            def product(lhsT, rhs, name, rows=P):
                for k in range(CT):
                    last = nc.tensor.matmul(prep_bank[0:rows, :], lhsT(k), rhs(k), start=(k == 0), stop=(k == CT - 1))
                last.then_inc(*pt.inc(name))

            def prep(b, s):
                if s == 5:
                    pe.wait_ge(pv.sem, pv.by(b, "xn"))
                    for c in range(CT):
                        prep_free(b, None if c == 0 else "xnT0")
                        transposes(prep_bank, lambda t, c=c: xn[:, t, c * P:(c + 1) * P], f"xnT{c}", pt)
                if s == 6:
                    for c in range(CT):
                        prep_free(b, f"xnT1" if c == 0 else "xp0")
                        product(lambda k, c=c: proj_sb[:, k, c * P:(c + 1) * P], lambda k: xnT[:, k, :], f"xp{c}")
                if s in (7, 8):
                    r = s - 7
                    for c in range(CT):
                        j = r * CT + c
                        prep_free(b, "xp1" if j == 0 else f"u{j - 1}")
                        product(lambda k, c=c: branch_sb[:, r, k, c * P:(c + 1) * P], lambda k: xpT[:, k, :], f"u{j}")
                if s == 9:
                    pe.wait_ge(pv.sem, pv.by(b, "z"))
                    for c in range(CT):
                        prep_free(b, "u3" if c == 0 else "zT0")
                        transposes(prep_bank, lambda t, c=c: z_sb[:, c, t * P:(t + 1) * P], f"zT{c}", pt)
                if s == 14:
                    pe.wait_ge(pv.sem, pv.by(b, "u"))
                    for r in range(BRANCHES):
                        prep_free(b, "zT1" if r == 0 else "db0")
                        product(lambda k: dbc_sb[:, k, 0:ROWS_B], lambda k, r=r: u_sb[:, r * CT + k, :], f"db{r}", ROWS_B)
                if s == 15:
                    prep_free(b, "db1")
                    for r in range(BRANCHES):
                        for k in range(CT):
                            last = nc.tensor.matmul(prep_bank[0:96, :], c_w[:, r, k, :], u_sb[:, r * CT + k, :],
                                                    start=(r == 0 and k == 0), stop=(r == BRANCHES - 1 and k == CT - 1))
                    last.then_inc(*pt.inc("c"))
                if s in (16, 17):
                    for j in (2 * (s - 16), 2 * (s - 16) + 1):
                        r, c = j // CT, j % CT
                        prep_free(b, "c" if j == 0 else f"d{j - 1}")
                        nc.tensor.matmul(prep_bank[:, :], dt_sb[:, c * P:(c + 1) * P], low[0:DT_RANK, r, :],
                                         start=True, stop=True).then_inc(*pt.inc(f"d{j}"))

            def add_transposed(src, c, first, last_unit):
                for t in range(TT):
                    col = (t % 2) * DIM + c * P
                    last = nc.tensor.matmul(y_bank[t // 2][:, col:col + P], src(t), ident[:, :],
                                            start=first and t % 2 == 0, stop=last_unit,
                                            is_transpose=True, skip_group_check=True)
                return last

            def scan(b, s):
                n, r = s // 2, s % 2
                if s == 0:
                    pe.wait_ge(pv.sem, pv.by(b, "c_lo"))
                if b > 0 or s > 0:
                    pe.wait_ge(yc_done, b * STATES * UNITS + s * CT)
                nc.tensor.matmul(c_bank[:, :], pick[:, STATES * r + n:STATES * r + n + 1].to_broadcast([96, P]),
                                 c_parts[:, b % 2, :], start=True, stop=True).then_inc(c_done, 1)
                if s == 0:
                    pe.wait_ge(pv.sem, pv.by(b, "ud"))
                    if b > 0:
                        pe.wait_ge(fve.sem, fve.by(b - 1, "yz1"))
                    for c in range(CT):
                        last = add_transposed(lambda t, c=c: ud[:, c, t * P:(t + 1) * P], c, c == 0, False)
                    last.then_inc(y_started, 1)
                for c in range(CT):
                    g = n * UNITS + r * CT + c
                    pe.wait_ge(yc_done, b * STATES * UNITS + g + 1)
                    add_transposed(lambda t: state[:, g % STATE_RING, t * P:(t + 1) * P], c, False,
                                   s == SLOTS - 1).then_inc(y_added, 1)

            def ffn(b, s):
                if s == 3:
                    pe.wait_ge(fve.sem, fve.by(b, "xf"))
                    for c in range(CT):
                        if c > 0:
                            pe.wait_ge(fs.sem, fs.by(b, "xfT0"))
                        elif b > 0:
                            pe.wait_ge(fs.sem, fs.by(b - 1, f"relu{2 * PAIRS - 1}"))
                        transposes(ffn_bank, lambda t, c=c: xf[:, t, c * P:(c + 1) * P], f"xfT{c}", fte)
                if s == 4:
                    pe.wait_ge(fs.sem, fs.by(b, "xfT1"))
                    for t in range(TT):
                        for k in range(CT):
                            last = nc.tensor.matmul(ffn_bank[:, t * EXPERTS:(t + 1) * EXPERTS],
                                                    xfT[:, k, t * P:(t + 1) * P], gate_sb[:, k, :],
                                                    start=(k == 0), stop=(k == CT - 1))
                    last.then_inc(*fte.inc("logits"))
                for m, up in enumerate(UP_SLOT):
                    half, q = m // PAIRS, m % PAIRS
                    if up == s:
                        pe.wait_ge(fs.sem, fs.by(b, "z_logits" if m == 0 else ("cwT" if m == 2 else f"relu{m - 1}")))
                        for j in range(2):
                            for k in range(CT):
                                if q < SHARED_PAIRS:
                                    w = sup_sb[:, k, (2 * q + j) * P:(2 * q + j + 1) * P]
                                else:
                                    e = 2 * (q - SHARED_PAIRS) + j
                                    w = up_sb[:, k, e * INTER:(e + 1) * INTER]
                                last = nc.tensor.matmul(ffn_bank[:, j * HALF:(j + 1) * HALF], w,
                                                        xfT[:, k, half * HALF:(half + 1) * HALF],
                                                        start=(k == 0), stop=(k == CT - 1))
                        last.then_inc(*fte.inc(f"up{m}"))
                    if up + 2 == s:
                        if q < SHARED_PAIRS:
                            pe.wait_ge(fs.sem, fs.by(b, f"square{m}"))
                        else:
                            pe.wait_ge(fve.sem, fve.by(b, f"weigh{m}"))
                        if q == 0:
                            if half > 0:
                                pe.wait_ge(fve.sem, fve.by(b, "out0"))
                            elif b > 0:
                                pe.wait_ge(fve.sem, fve.by(b - 1, "out1"))
                        for j in range(2):
                            w = sdown_sb[:, 2 * q + j, :] if q < SHARED_PAIRS else down_sb[:, 2 * (q - SHARED_PAIRS) + j, :]
                            for t in range(2):
                                last = nc.tensor.matmul(down_bank[:, t * DIM:(t + 1) * DIM],
                                                        hidden[:, m % 2, j, t * P:(t + 1) * P], w,
                                                        start=(q == 0 and j == 0 and t == 0),
                                                        stop=(q == PAIRS - 1 and j == 1), skip_group_check=True)
                        last.then_inc(*fte.inc(f"down{m}"))
                if s == 7:
                    pe.wait_ge(fve.sem, fve.by(b, f"route{ROUTER_STEPS - 1}"))
                    pe.wait_ge(fs.sem, fs.by(b, "relu1"))
                    for t in range(TT):
                        last = nc.tensor.transpose(ffn_bank[0:EXPERTS, t * P:(t + 1) * P],
                                                   r_w[:, t * EXPERTS:(t + 1) * EXPERTS], ident[:, :])
                    last.then_inc(*fte.inc("cwT"))

            run(pe, prep, scan, ffn)


_OUT = (BATCH, SEQ, DIM)


def kernel(**inputs):
    import numpy as np
    import concourse.bacc as bacc
    from concourse.bass_utils import run_bass_kernel_spmd

    def t(a):
        return np.ascontiguousarray(np.swapaxes(a, -1, -2))

    g = {k: np.asarray(v) for k, v in inputs.items()}
    A, F = "L0_attn_", "L0_ffn_"
    up = g[F + "up_w"]
    arrays = {
        "x": g[A + "x"], "ln_w": g[A + "ln_w"], "ln_b": g[A + "ln_b"],
        "projT": t(g[A + "proj_W"]), "proj_b": g[A + "proj_b"],
        "fT": t(g[A + "fconv_W"]), "f_b": g[A + "fconv_b"],
        "bT": t(g[A + "bconv_W"]), "b_b": g[A + "bconv_b"],
        "dbcT": t(g[A + "deltaBC_W"]), "dtT": t(g[A + "dt_W"]), "dt_b": g[A + "dt_b"],
        "A_log": g[A + "A_log"], "D": g[A + "D"],
        "gateT": t(g[F + "gate_w"]), "bias_e": g[F + "bias_e"],
        "upT": t(up.reshape(EXPERTS * INTER, DIM)), "downT": t(g[F + "down_w"]),
        "shared_upT": t(g[F + "shared_up"]), "shared_downT": t(g[F + "shared_down"]),
    }
    nc = bacc.Bacc("TRN2", target_bir_lowering=False, num_devices=1)
    args, data = [], {}
    for name, a in arrays.items():
        a = np.ascontiguousarray(a)
        data[f"{name}_dram"] = a
        args.append(nc.dram_tensor(f"{name}_dram", a.shape, mybir.dt.from_np(a.dtype), kind="ExternalInput").ap())
    args.append(nc.dram_tensor("out_dram", _OUT, mybir.dt.float32, kind="ExternalOutput").ap())
    block_kernel(nc, *args)
    r = run_bass_kernel_spmd(nc, [data], core_ids=[0])
    return r.results[0]["out_dram"]
```

```python
import concourse.bass as bass
from concourse import mybir
from contextlib import ExitStack

BATCH, SEQ, DIM = 8, 512, 256
STATES, DT_RANK = 16, 64
EXPERTS, INTER, SHARED = 16, 128, 512
GROUPS, TOP_GROUPS, TOP_K, ROUTED_SCALE = 4, 2, 4, 2.5
EPS = 1e-5
P = 128
TT = SEQ // P
CT = DIM // P
BRANCHES = 2
UNITS = BRANCHES * CT
SLOTS = 2 * STATES
HALF = SEQ // 2
SHARED_PAIRS = SHARED // P // 2
EXPERT_PAIRS = EXPERTS // 2
PAIRS = SHARED_PAIRS + EXPERT_PAIRS
ROWS_B = DT_RANK + STATES
SOFTPLUS_CLAMP = 40.0

PREP_PRODUCTS = {"xnT0": 0, "xnT1": 1, "xp0": 2, "xp1": 3, "u0": 4, "u1": 5, "u2": 6, "u3": 7,
                 "zT0": 9, "zT1": 11, "db0": 12, "d0": 13, "db1": 15, "d1": 16, "d2": 18, "d3": 20, "c": 22}
CLAMP, EXPONENT, LOWER, LOGARITHM, MAXIMUM = 2, 3, 4, 5, 6
Z_SLOTS = (5, 6, 7, 8)
B_STORE_SLOT, C_SPLIT_SLOT, UD_SLOT, LOAD_SLOT = 17, 24, 27, 12
NORM_SLOTS = (24, 25, 26, 27, 29)
UP_SLOT = [6, 8] + list(range(10, 28))
ROUTE_SLOT, CW_SLOT = 7, 9
OUT_SLOT = [UP_SLOT[PAIRS - 1] + 4, UP_SLOT[2 * PAIRS - 1] + 4]
assert len(UP_SLOT) == 2 * PAIRS and OUT_SLOT[1] < SLOTS

STATE_RING, B_RING, CW_RING = 8, 4, 4
POOL_LEAD = 2


def softplus_at(slot, after):
    return [(tag, j) for tag in "du" for j in range(UNITS) if PREP_PRODUCTS[f"{tag}{j}"] + after == slot]


def pairs_at(slot, after, experts_only=False):
    return [m for m, up in enumerate(UP_SLOT) if up + after == slot
            and not (experts_only and m % PAIRS < SHARED_PAIRS)]


class Steps:

    def __init__(self, sem, names):
        self.sem, self.names, self.at = sem, names, 0

    def inc(self, name):
        assert self.names[self.at] == name, (name, self.names[self.at])
        self.at = (self.at + 1) % len(self.names)
        return self.sem, 1

    def by(self, b, name):
        return b * len(self.names) + (self.names.index(name) + 1)


def norm_steps(tag):
    return [f"{tag}_stats", f"{tag}_moments", f"{tag}_var", f"{tag}_y2", f"{tag}_vy2", f"{tag}_corr", f"{tag}_rstd"]


PREP_TENSOR = sorted(PREP_PRODUCTS, key=PREP_PRODUCTS.get)
PREP_SCALAR = []
PREP_VECTOR = ["xs"]
NORM_VECTOR = norm_steps("outer") + ["xl"] + norm_steps("inner") + ["xn"]
NORM_SCALAR = ["outer_ln", "outer_y", "inner_ln", "inner_y"]
PREP_POOL = []
ROUTER_STEPS = 26
FFN_VECTOR = ["yz0", "yz1", "x1"] + norm_steps("ffn") + ["xf"]
FFN_SCALAR = ["ffn_ln", "ffn_y", "xfT0", "xfT1", "z_logits"]
FFN_TENSOR = ["xfT0", "xfT1", "logits"]
FFN_POOL = []
for _slot in range(SLOTS):
    PREP_SCALAR += [name for name, at in PREP_PRODUCTS.items() if at + 1 == _slot]
    PREP_SCALAR += [name for name, at in zip(("z_exp", "z_ln", "z_sig"), Z_SLOTS) if at == _slot]
    PREP_SCALAR += [f"{tag}_exp{j}" for tag, j in softplus_at(_slot, EXPONENT)]
    PREP_SCALAR += [f"{tag}_ln{j}" for tag, j in softplus_at(_slot, LOGARITHM)]
    PREP_POOL += [f"{tag}_min{j}" for tag, j in softplus_at(_slot, CLAMP)]
    for _tag, _j in softplus_at(_slot, LOWER):
        PREP_POOL += [f"{_tag}_lin{_j}", f"{_tag}_low{_j}"]
    PREP_VECTOR += ["z"] if _slot == Z_SLOTS[3] else []
    for _tag, _j in softplus_at(_slot, MAXIMUM):
        PREP_VECTOR += [f"{_tag}_max{_j}", f"{_tag}{_j}"] + ([f"du{_j}"] if _tag == "d" else [])
    if _slot == C_SPLIT_SLOT:
        PREP_VECTOR += ["c_hi", "c_r1a", "c_r1b", "c_mid_a", "c_mid_b", "c_r2", "c_lo"]
    if _slot == UD_SLOT:
        PREP_VECTOR += ["ud_0", "ud"]
    if _slot == ROUTE_SLOT:
        FFN_VECTOR += [f"route{i}" for i in range(ROUTER_STEPS)]
    FFN_VECTOR += [f"out{half}" for half in range(2) if OUT_SLOT[half] == _slot]
    if _slot == CW_SLOT:
        FFN_TENSOR.append("cwT")
    if _slot == CW_SLOT + 1:
        FFN_SCALAR.append("cwT")
    FFN_TENSOR += [f"up{m}" for m in pairs_at(_slot, 0)] + [f"down{m}" for m in pairs_at(_slot, 3)]
    for _m in pairs_at(_slot, 1):
        FFN_SCALAR += [f"relu{_m}", f"square{_m}"]
    FFN_POOL += [f"weigh{m}" for m in pairs_at(_slot, 2, experts_only=True)]


def block_kernel(nc, x, ln_w, ln_b, projT, proj_b, fT, f_b, bT, b_b, dbcT, dtT, dt_b, A_log, D,
                 gateT, bias_e, upT, downT, shared_upT, shared_downT, out):
    f32, bf16 = mybir.dt.float32, mybir.dt.bfloat16
    ALU = mybir.AluOpType
    ACT = mybir.ActivationFunctionType
    AX = mybir.AxisListType

    with ExitStack() as ctx:
        def sb(name, shape, dt=f32):
            return ctx.enter_context(nc.sbuf_tensor(name, shape, dt))

        def bank(name):
            return ctx.enter_context(nc.psum_tensor(name, [P, SEQ], f32))

        def sem(name):
            return ctx.enter_context(nc.semaphore(name))

        b_dram = nc.dram_tensor("b_rows", [BATCH, BRANCHES, STATES, SEQ], f32, kind="Internal").ap()
        cw_dram = nc.dram_tensor("cw_rows", [BATCH, EXPERTS, SEQ], f32, kind="Internal").ap()

        proj_sb = sb("proj_sb", [P, CT, DIM])
        branch_sb = sb("branch_sb", [P, BRANCHES, CT, DIM])
        dbc_sb = sb("dbc_sb", [P, CT, ROWS_B + STATES])
        c_w = sb("c_w", [P, BRANCHES, CT, 96])
        dt_sb = sb("dt_sb", [DT_RANK, DIM])
        gate_sb = sb("gate_sb", [P, CT, EXPERTS])
        up_sb = sb("up_sb", [P, CT, EXPERTS * INTER])
        down_sb = sb("down_sb", [P, EXPERTS, DIM])
        sup_sb = sb("sup_sb", [P, CT, SHARED])
        sdown_sb = sb("sdown_sb", [P, SHARED // P, DIM])
        lnw_c, lnb_c, projb_c, dtb_c, d_c = [sb(n, [P, CT]) for n in ("lnw_c", "lnb_c", "projb_c", "dtb_c", "d_c")]
        branchb_c = sb("branchb_c", [P, BRANCHES, CT])
        neg_a = sb("neg_a", [P, CT, STATES])
        bias_sb = sb("bias_sb", [P, EXPERTS])
        ident = sb("ident", [P, P])
        pick = sb("pick", [96, 32], bf16)
        lower = sb("lower", [P, GROUPS, GROUPS])
        restart = sb("restart", [P, TT * EXPERTS])

        x_sb = sb("x_sb", [P, TT, DIM])
        xnT = x_sb[:, :, :].rearrange("p a b -> p (a b)").rearrange("p (c t) -> p c t", c=CT)
        xl = sb("xl", [P, TT, DIM])
        z_sb = xl[:, :, :].rearrange("p a b -> p (a b)").rearrange("p (c t) -> p c t", c=CT)
        xs = sb("xs", [P, 2, TT, DIM])
        zT = sb("zT", [P, 2, TT, DIM])
        xpT = sb("xpT", [P, CT, SEQ])
        pre = sb("pre", [P, UNITS, SEQ])
        ex = sb("ex", [P, UNITS, SEQ])
        xn = ex[:, 0:2, :].rearrange("p a b -> p (a b)").rearrange("p (c t) -> p c t", c=TT)
        u_sb = sb("u_sb", [P, UNITS, SEQ])
        ud = sb("ud", [P, CT, SEQ])
        delta = sb("delta", [P, 2, UNITS, SEQ])
        du = sb("du", [P, 2, UNITS, SEQ])
        low = sb("low", [ROWS_B, BRANCHES, SEQ])
        c_sb = xpT[0:96, 0, :]
        c_parts = sb("c_parts", [96, 2, SEQ], bf16)
        stats = sb("stats", [P, TT, 6])
        mv = sb("mv", [P, TT, 2])
        nv, ny, nt, nr = [sb(n, [P, TT]) for n in ("nv", "ny", "nt", "nr")]

        b_ring = sb("b_ring", [P, B_RING, BRANCHES, SEQ])
        state = sb("state", [P, STATE_RING, SEQ])

        x1 = sb("x1", [P, TT, DIM])
        act_sb = sb("act_sb", [P, 2, 2, HALF])
        xf = act_sb[:, :, :, :].rearrange("p a b c -> p a (b c)").rearrange("p a b -> p (a b)").rearrange(
            "p (c t) -> p c t", c=TT)
        xfT = sb("xfT", [P, CT, SEQ])
        hidden = sb("hidden", [P, 2, 2, HALF])
        cw_ring = sb("cw_ring", [P, CW_RING, 2, HALF])
        cwT = ud[0:EXPERTS, 0, :]
        out_sb = sb("out_sb", [P, 2, DIM])
        fstats = sb("fstats", [P, TT, 6])
        fmv = sb("fmv", [P, TT, 2])
        fv, fy, ft, fr = [sb(n, [P, TT]) for n in ("fv", "fy", "ft", "fr")]
        TE = TT * EXPERTS
        r_e, r_s, r_b, r_m, r_g, r_q, r_w = [sb(n, [P, TE]) for n in ("r_e", "r_s", "r_b", "r_m", "r_g", "r_q", "r_w")]
        r_hi, r_lo = [sb(n, [P, TE // 2]) for n in ("r_hi", "r_lo")]
        r_t1, r_t2, r_gs, r_gk = [sb(n, [P, TT * GROUPS]) for n in ("r_t1", "r_t2", "r_gs", "r_gk")]
        r_c1, r_c2 = [sb(n, [P, TT, GROUPS, GROUPS]) for n in ("r_c1", "r_c2")]
        r_top = sb("r_top", [P, TT, 8])
        r_n, r_sum = [sb(n, [P, TT]) for n in ("r_n", "r_sum")]

        prep_bank, ffn_bank, down_bank, c_bank = bank("prep_bank"), bank("ffn_bank"), bank("down_bank"), bank("c_bank")
        decay = [bank("decay0"), bank("decay1")]
        y_bank = [bank("y0"), bank("y1")]

        weights_in = sem("weights_in")
        experts_in = sem("experts_in")
        pool_consts = sem("pool_consts")
        vector_consts = sem("vector_consts")
        a_exp = sem("a_exp")
        x_in = sem("x_in")
        b_stored = sem("b_stored")
        b_in = [sem(f"b_in{i}") for i in range(B_RING)]
        cw_stored = sem("cw_stored")
        cw_in = [sem(f"cw_in{i}") for i in range(CW_RING)]
        out_stored = sem("out_stored")
        decay_done = sem("decay_done")
        input_done = sem("input_done")
        scan_done = sem("scan_done")
        yc_done = sem("yc_done")
        c_done = sem("c_done")
        y_started = sem("y_started")
        y_added = sem("y_added")
        pv = Steps(sem("prep_vector"), PREP_VECTOR)
        ps = Steps(sem("prep_scalar"), PREP_SCALAR)
        pt = Steps(sem("prep_tensor"), PREP_TENSOR)
        pp = Steps(sem("prep_pool"), PREP_POOL)
        fve = Steps(sem("ffn_vector"), FFN_VECTOR)
        fs = Steps(sem("ffn_scalar"), FFN_SCALAR)
        fte = Steps(sem("ffn_tensor"), FFN_TENSOR)
        nve = Steps(sem("norm_vector"), NORM_VECTOR)
        ns = Steps(sem("norm_scalar"), NORM_SCALAR)
        fp = Steps(sem("ffn_pool"), FFN_POOL)

        block = ctx.enter_context(nc.Block())

        def run(norm, prep, scan, ffn, scan_last=False, lead=0):
            for b in range(-2, BATCH + 1):
                if b == 0:
                    for s in range(lead):
                        scan(0, s)
                for s in range(SLOTS):
                    ahead = b * SLOTS + s + lead
                    if b >= 0 and not scan_last and ahead < BATCH * SLOTS:
                        scan(ahead // SLOTS, ahead % SLOTS)
                    if b >= 1:
                        ffn(b - 1, s)
                    if b >= -1 and b + 1 < BATCH:
                        prep(b + 1, s)
                    if b + 2 < BATCH:
                        norm(b + 2, s)
                    if 0 <= b < BATCH and scan_last:
                        scan(b, s)

        loads, late = [], []

        @block.sync
        def _(sp):
            def load(dst, src):
                loads.append(1)
                sp.dma_start(dst, src).then_inc(weights_in, 16)

            def load_x(b):
                if b > 0:
                    sp.wait_ge(pt.sem, pt.by(b - 1, "xp1"))
                sp.dma_start(x_sb[:, :, :], x[b, :, :].rearrange("(t p) c -> p t c", p=P)).then_inc(x_in, 16)

            def late_load(dst, src):
                late.append(1)
                sp.dma_start(dst, src).then_inc(experts_in, 16)

            load_x(0)
            with nc.allow_non_contiguous_dma(reason="a few columns of constants"):
                load(lnw_c[:, :], ln_w.rearrange("(c p) -> p c", p=P))
                load(lnb_c[:, :], ln_b.rearrange("(c p) -> p c", p=P))
                load(projb_c[:, :], proj_b.rearrange("(c p) -> p c", p=P))
                load(branchb_c[:, 0, :], f_b.rearrange("(c p) -> p c", p=P))
                load(branchb_c[:, 1, :], b_b.rearrange("(c p) -> p c", p=P))
                load(dtb_c[:, :], dt_b.rearrange("(c p) -> p c", p=P))
                load(d_c[:, :], D.rearrange("(c p) -> p c", p=P))
            load(neg_a[:, :, :], A_log.rearrange("(c p) n -> p c n", p=P))
            load(proj_sb[:, :, :], projT.rearrange("(c p) n -> p c n", p=P))
            load(branch_sb[:, 0, :, :], fT.rearrange("(c p) n -> p c n", p=P))
            load(branch_sb[:, 1, :, :], bT.rearrange("(c p) n -> p c n", p=P))
            load(dbc_sb[:, :, :], dbcT.rearrange("(c p) n -> p c n", p=P))
            load(dt_sb[:, :], dtT)
            late_load(gate_sb[:, :, :], gateT.rearrange("(c p) n -> p c n", p=P))
            late_load(bias_sb[:, :], bias_e.partition_broadcast(P))
            late_load(sup_sb[:, :, :], shared_upT.rearrange("(c p) n -> p c n", p=P))
            late_load(sdown_sb[:, :, :], shared_downT.rearrange("(c p) n -> p c n", p=P))
            late_load(up_sb[:, :, :], upT.rearrange("(c p) n -> p c n", p=P))
            late_load(down_sb[:, :, :], downT.rearrange("e p n -> p e n"))

            def load_b(b, n):
                step = b * STATES + n
                if step >= B_RING:
                    sp.wait_ge(input_done, UNITS * (step - B_RING + 1))
                sp.wait_ge(b_stored, 16 * BRANCHES * (b + 1))
                sp.dma_start(b_ring[:, n % B_RING, :, :],
                             b_dram[b, :, n, :].partition_broadcast(P)).then_inc(b_in[n % B_RING], 16)

            def prep(b, s):
                if s == B_STORE_SLOT:
                    for r in range(BRANCHES):
                        sp.wait_ge(ps.sem, ps.by(b, f"db{r}"))
                        sp.dma_start(b_dram[b, r, :, :], low[DT_RANK:ROWS_B, r, :]).then_inc(b_stored, 16)
                if s == LOAD_SLOT and b + 1 < BATCH:
                    load_x(b + 1)
                if b == 0 and s == SLOTS - 1:
                    for n in range(B_RING - 1):
                        load_b(0, n)

            def scan(b, s):
                if s % 2 == 0:
                    n = s // 2 + B_RING - 1
                    if n < STATES:
                        load_b(b, n)
                    elif b + 1 < BATCH:
                        load_b(b + 1, n - STATES)

            def ffn(b, s):
                if s == CW_SLOT + 1:
                    sp.wait_ge(fs.sem, fs.by(b, "cwT"))
                    sp.dma_start(cw_dram[b, :, :], cwT).then_inc(cw_stored, 16)
                for m in pairs_at(s, 0, experts_only=True):
                    half, k = m // PAIRS, m % PAIRS - SHARED_PAIRS
                    before = (half * EXPERT_PAIRS + k) - CW_RING
                    if b > 0 or before >= 0:
                        b_, i = (b, before) if before >= 0 else (b - 1, before + 2 * EXPERT_PAIRS)
                        sp.wait_ge(fp.sem, fp.by(b_, f"weigh{(i // EXPERT_PAIRS) * PAIRS + SHARED_PAIRS + i % EXPERT_PAIRS}"))
                    sp.wait_ge(cw_stored, 16 * (b + 1))
                    sp.dma_start(cw_ring[:, k % CW_RING, :, :],
                                 cw_dram[b, 2 * k:2 * k + 2, half * HALF:(half + 1) * HALF].partition_broadcast(P)
                                 ).then_inc(cw_in[k % CW_RING], 16)
                for half in range(2):
                    if OUT_SLOT[half] == s:
                        sp.wait_ge(fve.sem, fve.by(b, f"out{half}"))
                        sp.dma_start(out[b, half * HALF:(half + 1) * HALF, :].rearrange("(t p) c -> p t c", p=P),
                                     out_sb[:, :, :]).then_inc(out_stored, 16)

            run(lambda b, s: None, prep, scan, ffn)
            sp.wait_ge(out_stored, 16 * 2 * BATCH)

        WEIGHTS, EXPERT_WEIGHTS = 16 * len(loads), 16 * len(late)

        @block.gpsimd
        def _(pool):
            nc.gpsimd.memset(ident[:, :], 0.0).then_inc(pool_consts, 1)
            nc.gpsimd.memset(pick[:, :], 0.0).then_inc(pool_consts, 1)
            nc.gpsimd.memset(lower[:, :, :], 1.0).then_inc(pool_consts, 1)
            pool.wait_ge(pool_consts, 3)
            nc.gpsimd.affine_select(out=ident[:, :], in_=ident[:, :], compare_op=ALU.not_equal, fill=1.0,
                                    base=0, pattern=[[-1, P]], channel_multiplier=1).then_inc(pool_consts, 1)
            nc.gpsimd.affine_select(out=lower[:, :, :], in_=lower[:, :, :], compare_op=ALU.is_gt, fill=0.0,
                                    base=0, pattern=[[1, GROUPS], [-1, GROUPS]], channel_multiplier=0
                                    ).then_inc(pool_consts, 1)
            for part in range(3):
                pool.wait_ge(pool_consts, 5 + part)
                nc.gpsimd.affine_select(out=pick[:, :], in_=pick[:, :], compare_op=ALU.not_equal, fill=1.0,
                                        base=-32 * part, pattern=[[-1, 32]], channel_multiplier=1
                                        ).then_inc(pool_consts, 1)

            def softplus_dst(b, tag, j):
                return u_sb[:, j, :] if tag == "u" else delta[:, b % 2, j, :]

            def prep(b, s):
                for tag, j in softplus_at(s, CLAMP):
                    pool.wait_ge(ps.sem, ps.by(b, f"{tag}{j}"))
                    if tag == "u":
                        pool.wait_ge(pt.sem, pt.by(b, "xnT1"))
                    else:
                        pool.wait_ge(pv.sem, pv.by(b, f"u_max{j}"))
                    nc.gpsimd.tensor_scalar(ex[:, j, :], pre[:, j, :], SOFTPLUS_CLAMP, -3.0e38, ALU.min, ALU.max
                                            ).then_inc(*pp.inc(f"{tag}_min{j}"))
                for tag, j in softplus_at(s, LOWER):
                    dst = softplus_dst(b, tag, j)
                    if tag == "u" and j == 0 and b > 0:
                        pool.wait_ge(pv.sem, pv.by(b - 1, "ud"))
                        pool.wait_ge(pt.sem, pt.by(b - 1, "c"))
                    if tag == "d" and j == 0 and b > 1:
                        pool.wait_ge(decay_done, UNITS * STATES * (b - 1))
                        pool.wait_ge(pv.sem, pv.by(b - 2, f"du{UNITS - 1}"))
                    pool.wait_ge(ps.sem, ps.by(b, f"{tag}_exp{j}"))
                    nc.gpsimd.tensor_scalar(dst, ex[:, j, :], -0.5, 1.0, ALU.mult, ALU.add
                                            ).then_inc(*pp.inc(f"{tag}_lin{j}"))
                    pool.wait_ge(pp.sem, pp.by(b, f"{tag}_lin{j}"))
                    nc.gpsimd.tensor_tensor(dst, dst, ex[:, j, :], ALU.mult).then_inc(*pp.inc(f"{tag}_low{j}"))

            def ffn(b, s):
                for m in pairs_at(s, 2, experts_only=True):
                    half, k = m // PAIRS, m % PAIRS - SHARED_PAIRS
                    pool.wait_ge(fte.sem, fte.by(b, f"down{m - 2}"))
                    uses = half * (EXPERT_PAIRS // CW_RING) + k // CW_RING + 1
                    pool.wait_ge(cw_in[k % CW_RING], 16 * (b * (2 * EXPERT_PAIRS // CW_RING) + uses))
                    pool.wait_ge(fs.sem, fs.by(b, f"square{m}"))
                    nc.gpsimd.tensor_tensor(hidden[:, m % 2, :, :], act_sb[:, m % 2, :, :],
                                            cw_ring[:, k % CW_RING, :, :], ALU.mult).then_inc(*fp.inc(f"weigh{m}"))

            def scan(b, s):
                n = s // 2
                for j in (2 * (s % 2), 2 * (s % 2) + 1):
                    g = n * UNITS + j
                    r = j // CT
                    if g == 0:
                        pool.wait_ge(pv.sem, pv.by(b, f"du{UNITS - 1}"))
                    if j == 0:
                        step = b * STATES + n
                        pool.wait_ge(b_in[n % B_RING], 16 * (step // B_RING + 1))
                    if b * STATES * UNITS + g >= STATE_RING:
                        pool.wait_ge(y_added, b * STATES * UNITS + g - STATE_RING + 1)
                    nc.gpsimd.tensor_tensor(state[:, g % STATE_RING, :], du[:, b % 2, j, :],
                                            b_ring[:, n % B_RING, r, :], ALU.mult).then_inc(input_done, 1)

            run(lambda b, s: None, prep, scan, ffn, lead=POOL_LEAD)

        @block.scalar
        def _(act):
            nc.scalar.preload_act_table_set("natural_log_exp_and_others")
            act.wait_ge(weights_in, WEIGHTS)
            nc.scalar.activation(neg_a[:, :, :], neg_a[:, :, :], ACT.Exp).then_inc(a_exp, 1)

            def rsqrt_guess(b, steps, vsteps, tag, v, y):
                act.wait_ge(vsteps.sem, vsteps.by(b, f"{tag}_var"))
                nc.scalar.activation(y[:, :], v[:, :], ACT.Ln).then_inc(*steps.inc(f"{tag}_ln"))
                act.wait_ge(steps.sem, steps.by(b, f"{tag}_ln"))
                nc.scalar.activation(y[:, :], y[:, :], ACT.Exp, scale=-0.5).then_inc(*steps.inc(f"{tag}_y"))

            def evacuate(b, name, dst, bias=0.0, scale=1.0, src=None):
                act.wait_ge(pt.sem, pt.by(b, name))
                nc.scalar.activation(dst, prep_bank[:, :] if src is None else src, ACT.Identity, bias=bias,
                                     scale=scale).then_inc(*ps.inc(name))

            def norm(b, s):
                if s == NORM_SLOTS[1]:
                    rsqrt_guess(b, ns, nve, "outer", nv, ny)
                if s == NORM_SLOTS[3]:
                    rsqrt_guess(b, ns, nve, "inner", nv, ny)

            def copy_out(b, name):
                kind, j = name.rstrip("0123"), int(name[-1]) if name[-1].isdigit() else 0
                c, r = j % CT, j // CT
                if kind == "xnT":
                    act.wait_ge(pv.sem, pv.by(b, "xs"))
                    evacuate(b, name, xnT[:, j, :], lnb_c[:, j:j + 1], lnw_c[:, j:j + 1])
                elif kind == "xp":
                    if b > 0:
                        act.wait_ge(pv.sem, pv.by(b - 1, "c_lo"))
                    evacuate(b, name, xpT[:, j, :], projb_c[:, j:j + 1])
                elif kind == "u":
                    if b > 0 and j == 0:
                        act.wait_ge(pv.sem, pv.by(b - 1, f"d{UNITS - 1}"))
                    evacuate(b, name, pre[:, j, :], branchb_c[:, r, c:c + 1])
                elif kind == "zT":
                    if b > 1 and j == 0:
                        act.wait_ge(fve.sem, fve.by(b - 2, "yz1"))
                    evacuate(b, name, zT[:, b % 2, :, j * P:(j + 1) * P],
                             src=prep_bank[:, :].rearrange("p (t c) -> p t c", t=TT))
                elif kind == "db":
                    if b > 0 and j == 0:
                        act.wait_ge(b_stored, 16 * BRANCHES * b)
                        act.wait_ge(pt.sem, pt.by(b - 1, "d3"))
                    evacuate(b, name, low[:, j, :], src=prep_bank[0:ROWS_B, :])
                elif kind == "d":
                    act.wait_ge(pv.sem, pv.by(b, f"u{j}"))
                    evacuate(b, name, pre[:, j, :], dtb_c[:, c:c + 1])
                else:
                    act.wait_ge(pv.sem, pv.by(b, "z"))
                    act.wait_ge(pt.sem, pt.by(b, "u3"))
                    evacuate(b, name, c_sb, src=prep_bank[0:96, :])

            def prep(b, s):
                for name, at in PREP_PRODUCTS.items():
                    if at + 1 == s:
                        copy_out(b, name)
                if s == Z_SLOTS[0]:
                    act.wait_ge(nve.sem, nve.by(b, "xn"))
                    act.wait_ge(pv.sem, pv.by(b, "xs"))
                    act.wait_ge(ps.sem, ps.by(b, "xp1"))
                    nc.scalar.activation(z_sb, xpT[:, :, :], ACT.Exp, scale=-1.0).then_inc(*ps.inc("z_exp"))
                if s == Z_SLOTS[1]:
                    act.wait_ge(ps.sem, ps.by(b, "z_exp"))
                    nc.scalar.activation(z_sb, z_sb, ACT.Ln, bias=1.0).then_inc(*ps.inc("z_ln"))
                if s == Z_SLOTS[2]:
                    act.wait_ge(ps.sem, ps.by(b, "z_ln"))
                    nc.scalar.activation(z_sb, z_sb, ACT.Exp, scale=-1.0).then_inc(*ps.inc("z_sig"))
                for tag, j in softplus_at(s, EXPONENT):
                    act.wait_ge(pp.sem, pp.by(b, f"{tag}_min{j}"))
                    nc.scalar.activation(ex[:, j, :], ex[:, j, :], ACT.Exp).then_inc(*ps.inc(f"{tag}_exp{j}"))
                for tag, j in softplus_at(s, LOGARITHM):
                    act.wait_ge(pp.sem, pp.by(b, f"{tag}_low{j}"))
                    nc.scalar.activation(ex[:, j, :], ex[:, j, :], ACT.Ln, bias=1.0).then_inc(*ps.inc(f"{tag}_ln{j}"))

            def scan(b, s):
                n = s // 2
                for j in (2 * (s % 2), 2 * (s % 2) + 1):
                    g = n * UNITS + j
                    total = b * STATES * UNITS + g
                    if g == 0:
                        act.wait_ge(pv.sem, pv.by(b, f"d{UNITS - 1}"))
                        if b == 0:
                            act.wait_ge(vector_consts, 2)
                    if total >= 2:
                        act.wait_ge(scan_done, total - 1)
                    nc.scalar.activation(decay[g % 2][:, :], delta[:, b % 2, j, :], ACT.Exp,
                                         scale=neg_a[:, j % CT, n:n + 1]).then_inc(decay_done, 1)

            def ffn(b, s):
                if s == 1:
                    rsqrt_guess(b, fs, fve, "ffn", fv, fy)
                if s in (4, 5):
                    c = s - 4
                    act.wait_ge(fte.sem, fte.by(b, f"xfT{c}"))
                    if b > 0 and c == 0:
                        act.wait_ge(fte.sem, fte.by(b - 1, f"up{2 * PAIRS - 1}"))
                    nc.scalar.activation(xfT[:, c, :], ffn_bank[:, :], ACT.Identity).then_inc(*fs.inc(f"xfT{c}"))
                if s == 6:
                    act.wait_ge(fte.sem, fte.by(b, "logits"))
                    nc.scalar.activation(r_e[:, :], ffn_bank[:, 0:TE], ACT.Exp, scale=-1.0).then_inc(*fs.inc("z_logits"))
                if s == CW_SLOT + 1:
                    act.wait_ge(fte.sem, fte.by(b, "cwT"))
                    act.wait_ge(y_started, min(b + 2, BATCH))
                    nc.scalar.activation(cwT, ffn_bank[0:EXPERTS, :], ACT.Identity).then_inc(*fs.inc("cwT"))
                for m in pairs_at(s, 1):
                    shared = m % PAIRS < SHARED_PAIRS
                    if m >= 2 and (m - 2) % PAIRS >= SHARED_PAIRS:
                        act.wait_ge(fp.sem, fp.by(b, f"weigh{m - 2}"))
                    elif m < 2 and b > 0:
                        act.wait_ge(fp.sem, fp.by(b - 1, f"weigh{2 * PAIRS - 2 + m}"))
                    act.wait_ge(fte.sem, fte.by(b, f"up{m}"))
                    a = act_sb[:, m % 2, :, :].rearrange("p a b -> p (a b)")
                    nc.scalar.activation(a, ffn_bank[:, :], ACT.Relu).then_inc(*fs.inc(f"relu{m}"))
                    if shared:
                        if m >= 2:
                            act.wait_ge(fte.sem, fte.by(b, f"down{m - 2}"))
                        elif b > 0:
                            act.wait_ge(fte.sem, fte.by(b - 1, f"down{2 * PAIRS - 2 + m}"))
                    act.wait_ge(fs.sem, fs.by(b, f"relu{m}"))
                    dst = hidden[:, m % 2, :, :].rearrange("p a b -> p (a b)") if shared else a
                    nc.scalar.activation(dst, a, ACT.Square).then_inc(*fs.inc(f"square{m}"))

            run(norm, prep, scan, ffn)

        @block.vector
        def _(dve):
            dve.wait_ge(weights_in, WEIGHTS)
            dve.wait_ge(a_exp, 1)
            nc.vector.tensor_scalar(neg_a[:, :, :], neg_a[:, :, :], -1.0, None, ALU.mult).then_inc(vector_consts, 1)
            nc.vector.memset(c_w[:, :, :, :], 0.0).then_inc(vector_consts, 1)
            nc.vector.memset(restart[:, :], 1.0).then_inc(vector_consts, 1)
            dve.wait_ge(vector_consts, 3)
            nc.vector.memset(restart[:, :].rearrange("p (t e) -> p t e", e=EXPERTS)[:, :, 0:1], 0.0
                             ).then_inc(vector_consts, 1)
            for r in range(BRANCHES):
                for part in range(3):
                    col = 32 * part + STATES * r
                    nc.vector.tensor_copy(c_w[:, r, :, col:col + STATES], dbc_sb[:, :, ROWS_B:ROWS_B + STATES]
                                          ).then_inc(vector_consts, 1)
            dve.wait_ge(pool_consts, 8)
            dve.wait_ge(vector_consts, 4 + 3 * BRANCHES)

            def norm_moments(b, steps, tag, src, st, m, v):
                for t in range(TT):
                    last = nc.vector.bn_stats(st[:, t, :], src[:, t, :])
                last.then_inc(*steps.inc(f"{tag}_stats"))
                dve.wait_ge(steps.sem, steps.by(b, f"{tag}_stats"))
                for t in range(TT):
                    last = nc.vector.bn_aggr(m[:, t, :], st[:, t, :])
                last.then_inc(*steps.inc(f"{tag}_moments"))
                dve.wait_ge(steps.sem, steps.by(b, f"{tag}_moments"))
                nc.vector.tensor_scalar(v[:, :], m[:, :, 1], EPS, None, ALU.add).then_inc(*steps.inc(f"{tag}_var"))

            def norm_apply(b, steps, ssteps, tag, dst, src, m, v, y, t_, r_, done):
                dve.wait_ge(ssteps.sem, ssteps.by(b, f"{tag}_y"))
                nc.vector.tensor_tensor(t_[:, :], y[:, :], y[:, :], ALU.mult).then_inc(*steps.inc(f"{tag}_y2"))
                dve.wait_ge(steps.sem, steps.by(b, f"{tag}_y2"))
                nc.vector.tensor_tensor(t_[:, :], t_[:, :], v[:, :], ALU.mult).then_inc(*steps.inc(f"{tag}_vy2"))
                dve.wait_ge(steps.sem, steps.by(b, f"{tag}_vy2"))
                nc.vector.tensor_scalar(t_[:, :], t_[:, :], -0.5, 1.5, ALU.mult, ALU.add
                                        ).then_inc(*steps.inc(f"{tag}_corr"))
                dve.wait_ge(steps.sem, steps.by(b, f"{tag}_corr"))
                nc.vector.tensor_tensor(r_[:, :], y[:, :], t_[:, :], ALU.mult).then_inc(*steps.inc(f"{tag}_rstd"))
                dve.wait_ge(steps.sem, steps.by(b, f"{tag}_rstd"))
                for t in range(TT):
                    last = nc.vector.tensor_scalar(dst[:, t, :], src[:, t, :], m[:, t, 0:1], r_[:, t:t + 1],
                                                   ALU.subtract, ALU.mult)
                last.then_inc(*steps.inc(done))

            def norm(b, s):
                if s == NORM_SLOTS[0]:
                    dve.wait_ge(x_in, 16 * (b + 1))
                    norm_moments(b, nve, "outer", x_sb, stats, mv, nv)
                if s == NORM_SLOTS[2]:
                    if b > 0:
                        dve.wait_ge(pt.sem, pt.by(b - 1, "zT1"))
                    norm_apply(b, nve, ns, "outer", xl, x_sb, mv, nv, ny, nt, nr, "xl")
                    dve.wait_ge(nve.sem, nve.by(b, "xl"))
                    norm_moments(b, nve, "inner", xl, stats, mv, nv)
                if s == NORM_SLOTS[4]:
                    if b > 0:
                        dve.wait_ge(pv.sem, pv.by(b - 1, f"d{UNITS - 1}"))
                    norm_apply(b, nve, ns, "inner", xn, xl, mv, nv, ny, nt, nr, "xn")

            def prep(b, s):
                if s == 0:
                    dve.wait_ge(nve.sem, nve.by(b, "xl"))
                    if b > 1:
                        dve.wait_ge(fve.sem, fve.by(b - 2, "x1"))
                    nc.vector.tensor_tensor(xs[:, b % 2, :, :], x_sb[:, :, :], xl[:, :, :], ALU.add
                                            ).then_inc(*pv.inc("xs"))
                if s == Z_SLOTS[3]:
                    dve.wait_ge(ps.sem, ps.by(b, "z_sig"))
                    nc.vector.tensor_tensor(z_sb, z_sb, xpT[:, :, :], ALU.mult).then_inc(*pv.inc("z"))
                for tag, j in softplus_at(s, MAXIMUM):
                    dst = u_sb[:, j, :] if tag == "u" else delta[:, b % 2, j, :]
                    dve.wait_ge(ps.sem, ps.by(b, f"{tag}_ln{j}"))
                    nc.vector.tensor_tensor(pre[:, j, :], pre[:, j, :], ex[:, j, :], ALU.max
                                            ).then_inc(*pv.inc(f"{tag}_max{j}"))
                    dve.wait_ge(pv.sem, pv.by(b, f"{tag}_max{j}"))
                    nc.vector.tensor_tensor(dst, dst, pre[:, j, :], ALU.max).then_inc(*pv.inc(f"{tag}{j}"))
                    if tag == "d":
                        dve.wait_ge(pv.sem, pv.by(b, f"d{j}"))
                        if b > 1 and j == 0:
                            dve.wait_ge(input_done, UNITS * STATES * (b - 1))
                        nc.vector.tensor_tensor(du[:, b % 2, j, :], dst, u_sb[:, j, :], ALU.mult
                                                ).then_inc(*pv.inc(f"du{j}"))
                if s == C_SPLIT_SLOT:
                    dve.wait_ge(ps.sem, ps.by(b, "c"))
                    part = c_parts[:, b % 2, :]
                    nc.vector.tensor_copy(part, c_sb).then_inc(*pv.inc("c_hi"))
                    dve.wait_ge(pv.sem, pv.by(b, "c_hi"))
                    for rows, name in ((slice(32, 64), "c_r1a"), (slice(64, 96), "c_r1b")):
                        nc.vector.tensor_tensor(c_sb[rows, :], c_sb[rows, :], c_parts[rows, b % 2, :], ALU.subtract
                                                ).then_inc(*pv.inc(name))
                    dve.wait_ge(pv.sem, pv.by(b, "c_r1b"))
                    for rows, name in ((slice(32, 64), "c_mid_a"), (slice(64, 96), "c_mid_b")):
                        nc.vector.tensor_copy(c_parts[rows, b % 2, :], c_sb[rows, :]).then_inc(*pv.inc(name))
                    dve.wait_ge(pv.sem, pv.by(b, "c_mid_b"))
                    nc.vector.tensor_tensor(c_sb[64:96, :], c_sb[64:96, :], c_parts[64:96, b % 2, :], ALU.subtract
                                            ).then_inc(*pv.inc("c_r2"))
                    dve.wait_ge(pv.sem, pv.by(b, "c_r2"))
                    nc.vector.tensor_copy(c_parts[64:96, b % 2, :], c_sb[64:96, :]).then_inc(*pv.inc("c_lo"))
                if s == UD_SLOT:
                    if b > 0:
                        dve.wait_ge(y_started, b)
                    if b > 1:
                        dve.wait_ge(cw_stored, 16 * (b - 1))
                    for c in range(CT):
                        last = nc.vector.tensor_scalar(ud[:, c, :], u_sb[:, c, :], d_c[:, c:c + 1], None, ALU.mult)
                    last.then_inc(*pv.inc("ud_0"))
                    dve.wait_ge(pv.sem, pv.by(b, "ud_0"))
                    for c in range(CT):
                        last = nc.vector.scalar_tensor_tensor(ud[:, c, :], u_sb[:, CT + c, :], d_c[:, c:c + 1],
                                                              ud[:, c, :], ALU.mult, ALU.add)
                    last.then_inc(*pv.inc("ud"))

            def scan(b, s):
                n = s // 2
                pair = (2 * (s % 2), 2 * (s % 2) + 1)
                for j in pair:
                    g = n * UNITS + j
                    total = b * STATES * UNITS + g
                    dve.wait_ge(decay_done, total + 1)
                    dve.wait_ge(input_done, total + 1)
                    slot = state[:, g % STATE_RING, :]
                    nc.vector.tensor_tensor_scan(slot, decay[g % 2][:, :], slot, 0.0, ALU.mult, ALU.add
                                                 ).then_inc(scan_done, 1)
                for j in pair:
                    g = n * UNITS + j
                    total = b * STATES * UNITS + g
                    if j % CT == 0:
                        dve.wait_ge(c_done, b * STATES * BRANCHES + n * BRANCHES + j // CT + 1)
                    dve.wait_ge(scan_done, total + 1)
                    slot = state[:, g % STATE_RING, :]
                    nc.vector.tensor_tensor(slot, slot, c_bank[:, :], ALU.mult).then_inc(yc_done, 1)

            def route(b):
                at = [0]

                def link(ins):
                    ins.then_inc(*fve.inc(f"route{at[0]}"))
                    dve.wait_ge(fve.sem, fve.by(b, f"route{at[0]}"))
                    at[0] += 1

                def te(tile):
                    return tile[:, :].rearrange("p (t e) -> p t e", e=EXPERTS)

                tt_ = nc.vector.tensor_tensor
                if b == 0:
                    dve.wait_ge(experts_in, EXPERT_WEIGHTS)
                dve.wait_ge(fs.sem, fs.by(b, "z_logits"))
                link(nc.vector.tensor_scalar(r_e[:, :], r_e[:, :], 1.0, None, ALU.add))
                link(nc.vector.reciprocal(r_s[:, :], r_e[:, :]))
                link(tt_(te(r_b), te(r_s), bias_sb[:, :].unsqueeze(1).to_broadcast([P, TT, EXPERTS]), ALU.add))
                two = r_b[:, :].rearrange("p (a b) -> p a b", b=2)
                tt_(r_hi[:, :], two[:, :, 0], two[:, :, 1], ALU.max)
                link(tt_(r_lo[:, :], two[:, :, 0], two[:, :, 1], ALU.min))
                hi = r_hi[:, :].rearrange("p (a b) -> p a b", b=2)
                lo = r_lo[:, :].rearrange("p (a b) -> p a b", b=2)
                tt_(r_gs[:, :], hi[:, :, 0], hi[:, :, 1], ALU.max)
                tt_(r_t1[:, :], hi[:, :, 0], hi[:, :, 1], ALU.min)
                link(tt_(r_t2[:, :], lo[:, :, 0], lo[:, :, 1], ALU.max))
                link(tt_(r_t1[:, :], r_t1[:, :], r_t2[:, :], ALU.max))
                link(tt_(r_gs[:, :], r_gs[:, :], r_t1[:, :], ALU.add))
                gs = r_gs[:, :].rearrange("p (t g) -> p t g", g=GROUPS)
                shape = [P, TT, GROUPS, GROUPS]
                own, other = gs.unsqueeze(3).to_broadcast(shape), gs.unsqueeze(2).to_broadcast(shape)
                tt_(r_c1[:, :, :, :], other, own, ALU.is_gt)
                link(tt_(r_c2[:, :, :, :], other, own, ALU.is_equal))
                link(tt_(r_c2[:, :, :, :], r_c2[:, :, :, :], lower[:, :, :].unsqueeze(1).to_broadcast(shape), ALU.mult))
                link(tt_(r_c1[:, :, :, :], r_c1[:, :, :, :], r_c2[:, :, :, :], ALU.add))
                link(nc.vector.tensor_reduce(r_gk[:, :], r_c1[:, :, :, :].rearrange("p t g h -> p (t g) h"), AX.X, ALU.add))
                link(nc.vector.tensor_scalar(r_gk[:, :], r_gk[:, :], float(TOP_GROUPS), None, ALU.is_lt))
                per = EXPERTS // GROUPS
                link(tt_(r_m[:, :].rearrange("p (g k) -> p g k", k=per), r_b[:, :].rearrange("p (g k) -> p g k", k=per),
                         r_gk[:, :].unsqueeze(2).to_broadcast([P, TT * GROUPS, per]), ALU.mult))
                for t in range(TT):
                    last = nc.vector.max(r_top[:, t, :], te(r_m)[:, t, :])
                link(last)
                fourth = r_top[:, :, TOP_K - 1:TOP_K].to_broadcast([P, TT, EXPERTS])
                tt_(te(r_g), te(r_m), fourth, ALU.is_gt)
                link(tt_(te(r_q), te(r_m), fourth, ALU.is_equal))
                link(nc.vector.tensor_reduce(r_n[:, :], te(r_g), AX.X, ALU.add))
                link(nc.vector.tensor_scalar(r_n[:, :], r_n[:, :], -1.0, float(TOP_K), ALU.mult, ALU.add))
                link(nc.vector.tensor_tensor_scan(r_m[:, :], restart[:, :], r_q[:, :], 0.0, ALU.mult, ALU.add))
                link(tt_(te(r_m), te(r_m), r_n[:, :].unsqueeze(2).to_broadcast([P, TT, EXPERTS]), ALU.is_le))
                link(tt_(r_q[:, :], r_q[:, :], r_m[:, :], ALU.mult))
                link(tt_(r_g[:, :], r_g[:, :], r_q[:, :], ALU.add))
                link(tt_(r_w[:, :], r_s[:, :], r_g[:, :], ALU.mult))
                link(nc.vector.tensor_reduce(r_sum[:, :], te(r_w), AX.X, ALU.add))
                link(nc.vector.tensor_scalar(r_sum[:, :], r_sum[:, :], 1e-20, None, ALU.add))
                link(nc.vector.reciprocal(r_sum[:, :], r_sum[:, :]))
                link(nc.vector.scalar_tensor_tensor(te(r_w), te(r_w), ROUTED_SCALE,
                                                    r_sum[:, :].unsqueeze(2).to_broadcast([P, TT, EXPERTS]),
                                                    ALU.mult, ALU.mult))
                assert at[0] == ROUTER_STEPS, at

            def ffn(b, s):
                if s == 0:
                    dve.wait_ge(y_added, UNITS * STATES * (b + 1))
                    if b > 0:
                        dve.wait_ge(fve.sem, fve.by(b - 1, "out1"))
                    for h in range(2):
                        nc.vector.tensor_tensor(x1[:, 2 * h:2 * h + 2, :], zT[:, b % 2, 2 * h:2 * h + 2, :],
                                                y_bank[h][:, :].rearrange("p (t c) -> p t c", t=2), ALU.mult
                                                ).then_inc(*fve.inc(f"yz{h}"))
                    dve.wait_ge(fve.sem, fve.by(b, "yz1"))
                    nc.vector.tensor_tensor(x1[:, :, :], x1[:, :, :], xs[:, b % 2, :, :], ALU.add
                                            ).then_inc(*fve.inc("x1"))
                    dve.wait_ge(fve.sem, fve.by(b, "x1"))
                    norm_moments(b, fve, "ffn", x1, fstats, fmv, fv)
                if s == 2:
                    norm_apply(b, fve, fs, "ffn", xf, x1, fmv, fv, fy, ft, fr, "xf")
                if s == ROUTE_SLOT:
                    route(b)
                for half in range(2):
                    if OUT_SLOT[half] == s:
                        dve.wait_ge(fte.sem, fte.by(b, f"down{(half + 1) * PAIRS - 1}"))
                        if b > 0 or half > 0:
                            dve.wait_ge(out_stored, 16 * (2 * b + half))
                        nc.vector.tensor_tensor(out_sb[:, :, :], x1[:, 2 * half:2 * half + 2, :],
                                                down_bank[:, :].rearrange("p (t c) -> p t c", t=2), ALU.add
                                                ).then_inc(*fve.inc(f"out{half}"))

            run(norm, prep, scan, ffn)

        @block.tensor
        def _(pe):
            pe.wait_ge(weights_in, WEIGHTS)
            pe.wait_ge(pool_consts, 8)
            pe.wait_ge(vector_consts, 4 + 3 * BRANCHES)

            def prep_free(b, name):
                i = PREP_TENSOR.index(name)
                if i > 0:
                    pe.wait_ge(ps.sem, ps.by(b, PREP_TENSOR[i - 1]))
                elif b > 0:
                    pe.wait_ge(ps.sem, ps.by(b - 1, PREP_TENSOR[-1]))

            def transposes(bank_, src, name, steps):
                for t in range(TT):
                    last = nc.tensor.transpose(bank_[:, t * P:(t + 1) * P], src(t), ident[:, :])
                last.then_inc(*steps.inc(name))

            def product(lhsT, rhs, name, rows=P):
                for k in range(CT):
                    last = nc.tensor.matmul(prep_bank[0:rows, :], lhsT(k), rhs(k), start=(k == 0), stop=(k == CT - 1))
                last.then_inc(*pt.inc(name))

            def prep(b, s):
                for name, at in PREP_PRODUCTS.items():
                    if at == s:
                        prep_free(b, name)
                        prep_product(b, name)

            def prep_product(b, name):
                kind, j = name.rstrip("0123"), int(name[-1]) if name[-1].isdigit() else 0
                c, r = j % CT, j // CT
                if kind == "xnT":
                    pe.wait_ge(nve.sem, nve.by(b, "xn"))
                    transposes(prep_bank, lambda t: xn[:, t, j * P:(j + 1) * P], name, pt)
                elif kind == "xp":
                    pe.wait_ge(ps.sem, ps.by(b, "xnT1"))
                    product(lambda k: proj_sb[:, k, j * P:(j + 1) * P], lambda k: xnT[:, k, :], name)
                elif kind == "u":
                    pe.wait_ge(ps.sem, ps.by(b, "xp1"))
                    product(lambda k: branch_sb[:, r, k, c * P:(c + 1) * P], lambda k: xpT[:, k, :], name)
                elif kind == "zT":
                    pe.wait_ge(pv.sem, pv.by(b, "z"))
                    transposes(prep_bank, lambda t: z_sb[:, j, t * P:(t + 1) * P], name, pt)
                elif kind == "db":
                    pe.wait_ge(pv.sem, pv.by(b, f"u{j * CT + CT - 1}"))
                    product(lambda k: dbc_sb[:, k, 0:ROWS_B], lambda k: u_sb[:, j * CT + k, :], name, ROWS_B)
                elif kind == "d":
                    pe.wait_ge(ps.sem, ps.by(b, f"db{r}"))
                    nc.tensor.matmul(prep_bank[:, :], dt_sb[:, c * P:(c + 1) * P], low[0:DT_RANK, r, :],
                                     start=True, stop=True).then_inc(*pt.inc(name))
                else:
                    pe.wait_ge(pv.sem, pv.by(b, f"u{UNITS - 1}"))
                    for q in range(BRANCHES):
                        for k in range(CT):
                            last = nc.tensor.matmul(prep_bank[0:96, :], c_w[:, q, k, :], u_sb[:, q * CT + k, :],
                                                    start=(q == 0 and k == 0), stop=(q == BRANCHES - 1 and k == CT - 1))
                    last.then_inc(*pt.inc(name))

            def add_transposed(src, c, first, last_unit):
                for t in range(TT):
                    col = (t % 2) * DIM + c * P
                    last = nc.tensor.matmul(y_bank[t // 2][:, col:col + P], src(t), ident[:, :],
                                            start=first and t % 2 == 0, stop=last_unit,
                                            is_transpose=True, skip_group_check=True)
                return last

            def broadcast_c(b, s):
                n, r = s // 2, s % 2
                if s == 0:
                    pe.wait_ge(pv.sem, pv.by(b, "c_lo"))
                if b > 0 or s > 0:
                    pe.wait_ge(yc_done, b * STATES * UNITS + s * CT)
                nc.tensor.matmul(c_bank[:, :], pick[:, STATES * r + n:STATES * r + n + 1].to_broadcast([96, P]),
                                 c_parts[:, b % 2, :], start=True, stop=True).then_inc(c_done, 1)

            def scan(b, s):
                n, r = s // 2, s % 2
                if s == 0:
                    if b == 0:
                        broadcast_c(0, 0)
                    pe.wait_ge(pv.sem, pv.by(b, "ud"))
                    if b > 0:
                        pe.wait_ge(fve.sem, fve.by(b - 1, "yz1"))
                    for c in range(CT):
                        last = add_transposed(lambda t, c=c: ud[:, c, t * P:(t + 1) * P], c, c == 0, False)
                    last.then_inc(y_started, 1)
                if s + 1 < SLOTS:
                    broadcast_c(b, s + 1)
                elif b + 1 < BATCH:
                    broadcast_c(b + 1, 0)
                for c in range(CT):
                    g = n * UNITS + r * CT + c
                    pe.wait_ge(yc_done, b * STATES * UNITS + g + 1)
                    add_transposed(lambda t: state[:, g % STATE_RING, t * P:(t + 1) * P], c, False,
                                   s == SLOTS - 1).then_inc(y_added, 1)

            def ffn(b, s):
                if s in (3, 4):
                    c = s - 3
                    pe.wait_ge(fve.sem, fve.by(b, "xf"))
                    if c > 0:
                        pe.wait_ge(fs.sem, fs.by(b, "xfT0"))
                    elif b > 0:
                        pe.wait_ge(fs.sem, fs.by(b - 1, f"relu{2 * PAIRS - 1}"))
                    transposes(ffn_bank, lambda t: xf[:, t, c * P:(c + 1) * P], f"xfT{c}", fte)
                if s == 5:
                    if b == 0:
                        pe.wait_ge(experts_in, EXPERT_WEIGHTS)
                    pe.wait_ge(fs.sem, fs.by(b, "xfT1"))
                    for t in range(TT):
                        for k in range(CT):
                            last = nc.tensor.matmul(ffn_bank[:, t * EXPERTS:(t + 1) * EXPERTS],
                                                    xfT[:, k, t * P:(t + 1) * P], gate_sb[:, k, :],
                                                    start=(k == 0), stop=(k == CT - 1))
                    last.then_inc(*fte.inc("logits"))
                if s == CW_SLOT:
                    pe.wait_ge(fve.sem, fve.by(b, f"route{ROUTER_STEPS - 1}"))
                    pe.wait_ge(fs.sem, fs.by(b, "relu1"))
                    for t in range(TT):
                        last = nc.tensor.transpose(ffn_bank[0:EXPERTS, t * P:(t + 1) * P],
                                                   r_w[:, t * EXPERTS:(t + 1) * EXPERTS], ident[:, :])
                    last.then_inc(*fte.inc("cwT"))
                for m in pairs_at(s, 0):
                    pe.wait_ge(fs.sem, fs.by(b, "z_logits" if m == 0 else ("cwT" if m == 2 else f"relu{m - 1}")))
                    half, q = m // PAIRS, m % PAIRS
                    for j in range(2):
                        for k in range(CT):
                            if q < SHARED_PAIRS:
                                w = sup_sb[:, k, (2 * q + j) * P:(2 * q + j + 1) * P]
                            else:
                                e = 2 * (q - SHARED_PAIRS) + j
                                w = up_sb[:, k, e * INTER:(e + 1) * INTER]
                            last = nc.tensor.matmul(ffn_bank[:, j * HALF:(j + 1) * HALF], w,
                                                    xfT[:, k, half * HALF:(half + 1) * HALF],
                                                    start=(k == 0), stop=(k == CT - 1))
                    last.then_inc(*fte.inc(f"up{m}"))
                for m in pairs_at(s, 3):
                    half, q = m // PAIRS, m % PAIRS
                    if q < SHARED_PAIRS:
                        pe.wait_ge(fs.sem, fs.by(b, f"square{m}"))
                    else:
                        pe.wait_ge(fp.sem, fp.by(b, f"weigh{m}"))
                    if q == 0:
                        if half > 0:
                            pe.wait_ge(fve.sem, fve.by(b, "out0"))
                        elif b > 0:
                            pe.wait_ge(fve.sem, fve.by(b - 1, "out1"))
                    for j in range(2):
                        w = sdown_sb[:, 2 * q + j, :] if q < SHARED_PAIRS else down_sb[:, 2 * (q - SHARED_PAIRS) + j, :]
                        for t in range(2):
                            last = nc.tensor.matmul(down_bank[:, t * DIM:(t + 1) * DIM],
                                                    hidden[:, m % 2, j, t * P:(t + 1) * P], w,
                                                    start=(q == 0 and j == 0 and t == 0),
                                                    stop=(q == PAIRS - 1 and j == 1), skip_group_check=True)
                    last.then_inc(*fte.inc(f"down{m}"))

            run(lambda b, s: None, prep, scan, ffn, scan_last=True)


_OUT = (BATCH, SEQ, DIM)


def kernel(**inputs):
    import numpy as np
    import concourse.bacc as bacc
    from concourse.bass_utils import run_bass_kernel_spmd

    def t(a):
        return np.ascontiguousarray(np.swapaxes(a, -1, -2))

    g = {k: np.asarray(v) for k, v in inputs.items()}
    A, F = "L0_attn_", "L0_ffn_"
    up = g[F + "up_w"]
    arrays = {
        "x": g[A + "x"], "ln_w": g[A + "ln_w"], "ln_b": g[A + "ln_b"],
        "projT": t(g[A + "proj_W"]), "proj_b": g[A + "proj_b"],
        "fT": t(g[A + "fconv_W"]), "f_b": g[A + "fconv_b"],
        "bT": t(g[A + "bconv_W"]), "b_b": g[A + "bconv_b"],
        "dbcT": t(g[A + "deltaBC_W"]), "dtT": t(g[A + "dt_W"]), "dt_b": g[A + "dt_b"],
        "A_log": g[A + "A_log"], "D": g[A + "D"],
        "gateT": t(g[F + "gate_w"]), "bias_e": g[F + "bias_e"],
        "upT": t(up.reshape(EXPERTS * INTER, DIM)), "downT": t(g[F + "down_w"]),
        "shared_upT": t(g[F + "shared_up"]), "shared_downT": t(g[F + "shared_down"]),
    }
    nc = bacc.Bacc("TRN2", target_bir_lowering=False, num_devices=1)
    args, data = [], {}
    for name, a in arrays.items():
        a = np.ascontiguousarray(a)
        data[f"{name}_dram"] = a
        args.append(nc.dram_tensor(f"{name}_dram", a.shape, mybir.dt.from_np(a.dtype), kind="ExternalInput").ap())
    args.append(nc.dram_tensor("out_dram", _OUT, mybir.dt.float32, kind="ExternalOutput").ap())
    block_kernel(nc, *args)
    r = run_bass_kernel_spmd(nc, [data], core_ids=[0])
    return r.results[0]["out_dram"]
```

```python
import concourse.bass as bass
from concourse import mybir
from contextlib import ExitStack

BATCH, SEQ, DIM = 8, 512, 256
STATES, DT_RANK = 16, 64
EXPERTS, INTER, SHARED = 16, 128, 512
GROUPS, TOP_GROUPS, TOP_K, ROUTED_SCALE = 4, 2, 4, 2.5
EPS = 1e-5
P = 128
TT = SEQ // P
CT = DIM // P
BRANCHES = 2
UNITS = BRANCHES * CT
SLOTS = 2 * STATES
HALF = SEQ // 2
SHARED_PAIRS = SHARED // P // 2
EXPERT_PAIRS = EXPERTS // 2
PAIRS = SHARED_PAIRS + EXPERT_PAIRS
ROW_C, ROW_B, ROW_C2 = DT_RANK, DT_RANK + STATES, DT_RANK + 2 * STATES
assert ROW_C2 + 2 * STATES == P

ONE_C_BANK = 6
PREP_PRODUCTS = {"xnT0": 0, "xnT1": 1, "xp0": 2, "xp1": 3, "u0": 4, "u1": 5, "u2": 6, "u3": 7, "zT0": 8,
                 "zT1": 9, "db0": 11, "d0": 12, "db1": 14, "d1": 13, "d2": 15, "d3": 18}
EXPONENT, LOWER, LOGARITHM, MAXIMUM = 2, 3, 4, 5
Z_SLOTS = (5, 6, 6, 6)
B_STORE_SLOT, C_SPLIT_SLOT, UD_SLOT, LOAD_SLOT = 22, 25, 24, 13
NORM_SLOTS = (21, 22, 23, 24, 24, 25, 26, 29)
UP_SLOT = [6, 7, 10, 11, 12, 13, 14, 15, 16, 17, 18, 19, 20, 21, 22, 23, 24, 25, 26, 27]
DOWN_SLOT = [9, 10, 13, 14, 15, 16, 17, 18, 19, 20, 21, 22, 23, 24, 25, 26, 27, 28, 29, 30]
HEAD_SLOTS, XFT_SLOTS, LOGITS_SLOT = (0, 1, 1, 3), (3, 4), 5
ROUTE_SLOTS, CW_SLOT = (6, 6, 6, 7), 8
OUT_SLOT = [DOWN_SLOT[PAIRS - 1] + 1, DOWN_SLOT[2 * PAIRS - 1] + 1]
assert len(UP_SLOT) == len(DOWN_SLOT) == 2 * PAIRS and OUT_SLOT[1] < SLOTS

STATE_RING, B_RING, CW_RING = 8, 4, 4
POOL_LEAD = 2
LOOP_FIRST, LOOP_END, LOOP_STEP = 2, BATCH - 2, 2


def softplus_at(slot, after):
    return [(tag, j) for tag in "du" for j in range(UNITS) if PREP_PRODUCTS[f"{tag}{j}"] + after == slot]


def is_expert(m):
    return m % PAIRS >= SHARED_PAIRS


def pairs_at(slot, after, experts_only=False):
    return [m for m, up in enumerate(UP_SLOT) if up + after == slot and (is_expert(m) or not experts_only)]


def downs_at(slot):
    return [m for m, down in enumerate(DOWN_SLOT) if down == slot]


class Sequence:

    def __init__(self, at, register=None):
        self.at, self.register = at, register

    def __add__(self, k):
        return Sequence(self.at + k, self.register)

    def __sub__(self, k):
        return self + -k

    def __mod__(self, k):
        assert self.register is None or LOOP_STEP % k == 0
        return self.at % k

    def __gt__(self, k):
        return self.at > k

    def times(self, k, plus=0):
        constant = k * self.at + plus
        return constant if self.register is None else self.register * k + constant

    def number(self):
        return self.times(1)


class Steps:

    def __init__(self, sem, names):
        self.sem, self.names, self.at = sem, names, 0

    def inc(self, name):
        assert self.names[self.at] == name, (name, self.names[self.at])
        self.at = (self.at + 1) % len(self.names)
        return self.sem, 1

    def by(self, b, name):
        return b.times(len(self.names), self.names.index(name) + 1)


def norm_steps(tag):
    return [f"{tag}_stats", f"{tag}_moments", f"{tag}_var", f"{tag}_y2", f"{tag}_vy2", f"{tag}_corr", f"{tag}_rstd",
            f"{tag}_bias"]


NORM_VECTOR = norm_steps("outer") + norm_steps("inner")
NORM_SCALAR = ["outer_ln", "outer_y", "xl", "inner_ln", "inner_y", "xn"]
PREP_TENSOR = sorted(PREP_PRODUCTS, key=PREP_PRODUCTS.get)
PREP_SCALAR, PREP_VECTOR, PREP_POOL = [], [], ["xs"]
ROUTE_STEPS = (7, 6, 8, 5)
FFN_VECTOR = ["yz0", "yz1", "x1"] + norm_steps("ffn")
FFN_SCALAR = ["ffn_ln", "ffn_y", "xf", "xfT0", "xfT1", "z_logits"]
FFN_TENSOR = ["xfT0", "xfT1", "logits"]
FFN_POOL = []
for _slot in range(SLOTS):
    for _name in [name for name, at in PREP_PRODUCTS.items() if at + 1 == _slot]:
        if _name.rstrip("0123") in ("u", "d"):
            PREP_SCALAR.append(f"abs_{_name}")
        PREP_SCALAR.append(_name)
    PREP_SCALAR += [name for name, at in zip(("z_exp", "z_ln", "z_sig"), Z_SLOTS) if at == _slot]
    for _tag, _j in softplus_at(_slot, EXPONENT):
        PREP_SCALAR += [f"{_tag}_exp{_j}", f"{_tag}_lin{_j}"]
    PREP_SCALAR += [f"{tag}_ln{j}" for tag, j in softplus_at(_slot, LOGARITHM)]
    PREP_POOL += ["z"] if _slot == Z_SLOTS[3] else []
    for _tag, _j in softplus_at(_slot, LOWER):
        PREP_POOL += [f"{_tag}_low{_j}"]
    for _tag, _j in softplus_at(_slot, MAXIMUM):
        PREP_VECTOR += [f"{_tag}_max{_j}", f"{_tag}{_j}"]
    PREP_POOL += [f"du{j}" for tag, j in softplus_at(_slot, MAXIMUM + 1) if tag == "d"]
    if _slot == C_SPLIT_SLOT:
        PREP_SCALAR.append("c_hi")
        PREP_VECTOR.append("c_r1")
    if _slot == C_SPLIT_SLOT + 1:
        PREP_SCALAR.append("c_mid")
        PREP_VECTOR.append("c_r2")
    if _slot == C_SPLIT_SLOT + 2:
        PREP_SCALAR.append("c_lo")
    if _slot == UD_SLOT:
        PREP_POOL.append("u_sum")
    if _slot == UD_SLOT + 1:
        PREP_SCALAR.append("ud")
    for _part, _at in enumerate(ROUTE_SLOTS):
        if _at == _slot:
            FFN_VECTOR += [f"route{_part}_{i}" for i in range(ROUTE_STEPS[_part])]
    FFN_VECTOR += [f"out{half}" for half in range(2) if OUT_SLOT[half] == _slot]
    if _slot == CW_SLOT:
        FFN_TENSOR.append("cwT")
    if _slot == CW_SLOT + 1:
        FFN_SCALAR.append("cwT")
    FFN_TENSOR += [f"up{m}" for m in pairs_at(_slot, 0)] + [f"down{m}" for m in downs_at(_slot)]
    for _m in pairs_at(_slot, 1):
        FFN_SCALAR += [f"relu{_m}"] + ([f"square{_m}"] if is_expert(_m) else [])
    FFN_SCALAR += [f"square{m}" for m in pairs_at(_slot, 2) if not is_expert(m)]
    FFN_POOL += [f"weigh{m}" for m in pairs_at(_slot, 2, experts_only=True)]


def block_kernel(nc, x, ln_w, ln_b, projT, proj_b, fT, f_b, bT, b_b, dbcT, dtT, dt_b, A_log, D,
                 gateT, bias_e, upT, downT, shared_upT, shared_downT, out):
    f32, bf16 = mybir.dt.float32, mybir.dt.bfloat16
    ALU = mybir.AluOpType
    ACT = mybir.ActivationFunctionType
    AX = mybir.AxisListType

    with ExitStack() as ctx:
        def sb(name, shape, dt=f32):
            return ctx.enter_context(nc.sbuf_tensor(name, shape, dt))

        def bank(name):
            return ctx.enter_context(nc.psum_tensor(name, [P, SEQ], f32))

        def sem(name):
            return ctx.enter_context(nc.semaphore(name))

        b_dram = nc.dram_tensor("b_rows", [2, BRANCHES, STATES, SEQ], f32, kind="Internal").ap()
        cw_dram = nc.dram_tensor("cw_rows", [2, EXPERTS, SEQ], f32, kind="Internal").ap()

        proj_sb = sb("proj_sb", [P, CT, DIM])
        branch_sb = sb("branch_sb", [P, BRANCHES, CT, DIM])
        dbc_sb = sb("dbc_sb", [P, CT, P])
        dt_sb = sb("dt_sb", [DT_RANK, DIM])
        gate_sb = sb("gate_sb", [P, CT, EXPERTS])
        up_sb = sb("up_sb", [P, CT, EXPERTS * INTER])
        down_sb = sb("down_sb", [P, EXPERTS, DIM])
        sup_sb = sb("sup_sb", [P, CT, SHARED])
        sdown_sb = sb("sdown_sb", [P, SHARED // P, DIM])
        lnw_c, lnb_c, projb_c, dtb_c, d_c = [sb(n, [P, CT]) for n in ("lnw_c", "lnb_c", "projb_c", "dtb_c", "d_c")]
        branchb_c = sb("branchb_c", [P, BRANCHES, CT])
        neg_a = sb("neg_a", [P, CT, STATES])
        bias_sb = sb("bias_sb", [P, EXPERTS])
        ident = sb("ident", [P, P])
        pick = sb("pick", [P, STATES], bf16)
        third = sb("third", [P, 1])
        carrier = sb("carrier", [P, 1])
        lower = sb("lower", [P, GROUPS, GROUPS])
        restart = sb("restart", [P, TT * EXPERTS])

        x_sb = sb("x_sb", [P, TT, DIM])
        xnT = x_sb[:, :, :].rearrange("p a b -> p (a b)").rearrange("p (c t) -> p c t", c=CT)
        xl = sb("xl", [P, TT, DIM])
        z_sb = xl[:, :, :].rearrange("p a b -> p (a b)").rearrange("p (c t) -> p c t", c=CT)
        xs = sb("xs", [P, 2, TT, DIM])
        zT = sb("zT", [P, 2, TT, DIM])
        xpT = sb("xpT", [P, CT, SEQ])
        pre = sb("pre", [P, UNITS, SEQ])
        ex = sb("ex", [P, UNITS, SEQ])
        xn = ex[:, 0:2, :].rearrange("p a b -> p (a b)").rearrange("p (c t) -> p c t", c=TT)
        u_sb = sb("u_sb", [P, UNITS, SEQ])
        ud = sb("ud", [P, CT, SEQ])
        delta = sb("delta", [P, 2, UNITS, SEQ])
        du = sb("du", [P, 2, UNITS, SEQ])
        low = sb("low", [P, BRANCHES, SEQ])
        c_parts = sb("c_parts", [P, 2, BRANCHES, SEQ], bf16)
        stats = sb("stats", [P, TT, 6])
        mv = sb("mv", [P, TT, 2])
        nv, ny, nt, nr, nb = [sb(n, [P, TT]) for n in ("nv", "ny", "nt", "nr", "nb")]

        b_ring = sb("b_ring", [P, B_RING, BRANCHES, SEQ])
        state = sb("state", [P, STATE_RING, SEQ])

        x1 = sb("x1", [P, TT, DIM])
        act_sb = sb("act_sb", [P, 2, 2, HALF])
        xf = act_sb[:, :, :, :].rearrange("p a b c -> p a (b c)").rearrange("p a b -> p (a b)").rearrange(
            "p (c t) -> p c t", c=TT)
        xfT = sb("xfT", [P, CT, SEQ])
        hidden = sb("hidden", [P, 2, 2, HALF])
        cw_ring = sb("cw_ring", [P, CW_RING, 2, HALF])
        cwT = ud[0:EXPERTS, 0, :]
        out_sb = sb("out_sb", [P, 2, DIM])
        fstats = sb("fstats", [P, TT, 6])
        fmv = sb("fmv", [P, TT, 2])
        fv, fy, ft, fr, fb = [sb(n, [P, TT]) for n in ("fv", "fy", "ft", "fr", "fb")]
        TE = TT * EXPERTS
        r_e, r_s, r_b, r_m, r_g, r_q, r_w = [sb(n, [P, TE]) for n in ("r_e", "r_s", "r_b", "r_m", "r_g", "r_q", "r_w")]
        r_hi, r_lo = [sb(n, [P, TE // 2]) for n in ("r_hi", "r_lo")]
        r_t1, r_t2, r_gs, r_gk = [sb(n, [P, TT * GROUPS]) for n in ("r_t1", "r_t2", "r_gs", "r_gk")]
        r_c1, r_c2 = [sb(n, [P, TT, GROUPS, GROUPS]) for n in ("r_c1", "r_c2")]
        r_top = sb("r_top", [P, TT, 8])
        r_n, r_sum = [sb(n, [P, TT]) for n in ("r_n", "r_sum")]

        prep_bank, ffn_bank, down_bank, c_bank = bank("prep_bank"), bank("ffn_bank"), bank("down_bank"), bank("c_bank")
        decay = [bank("decay0"), bank("decay1")]
        y_bank = [bank("y0"), bank("y1")]

        def c_bank_of(s):
            return down_bank if s % 2 and s < ONE_C_BANK else c_bank

        def product_bank(b, name):
            return down_bank if b.at == 0 and PREP_TENSOR.index(name) % 2 else prep_bank

        def up_bank(b, m):
            return prep_bank if b.at == BATCH - 1 and m % 2 else ffn_bank

        weights_in = sem("weights_in")
        experts_in = sem("experts_in")
        pool_consts = sem("pool_consts")
        vector_consts = sem("vector_consts")
        a_done = sem("a_done")
        x_in = sem("x_in")
        b_stored = sem("b_stored")
        b_in = [sem(f"b_in{i}") for i in range(B_RING)]
        cw_stored = sem("cw_stored")
        cw_in = [sem(f"cw_in{i}") for i in range(CW_RING)]
        out_stored = sem("out_stored")
        decay_done = sem("decay_done")
        input_done = sem("input_done")
        scan_done = sem("scan_done")
        yc_done = sem("yc_done")
        c_done = sem("c_done")
        y_started = sem("y_started")
        y_added = sem("y_added")
        pv = Steps(sem("prep_vector"), PREP_VECTOR)
        ps = Steps(sem("prep_scalar"), PREP_SCALAR)
        pt = Steps(sem("prep_tensor"), PREP_TENSOR)
        pp = Steps(sem("prep_pool"), PREP_POOL)
        fve = Steps(sem("ffn_vector"), FFN_VECTOR)
        fs = Steps(sem("ffn_scalar"), FFN_SCALAR)
        fte = Steps(sem("ffn_tensor"), FFN_TENSOR)
        nve = Steps(sem("norm_vector"), NORM_VECTOR)
        ns = Steps(sem("norm_scalar"), NORM_SCALAR)
        fp = Steps(sem("ffn_pool"), FFN_POOL)

        block = ctx.enter_context(nc.Block())

        def softplus_dst(b, tag, j):
            return u_sb[:, j, :] if tag == "u" else delta[:, b % 2, j, :]

        def run(engine, norm, prep, scan, ffn, scan_last=False, lead=0):

            def step(b):
                for s in range(SLOTS):
                    ahead = s + lead
                    if not scan_last and (0 <= b.at < BATCH - 1 or b.at == BATCH - 1 and ahead < SLOTS):
                        scan(b + ahead // SLOTS, ahead % SLOTS)
                    if 1 <= b.at <= BATCH:
                        ffn(b - 1, s)
                    if -1 <= b.at < BATCH - 1:
                        prep(b + 1, s)
                    if b.at + 2 < BATCH:
                        norm(b + 2, s)
                    if scan_last and 0 <= b.at < BATCH:
                        scan(b, s)

            for b in range(-2, LOOP_FIRST):
                if b == 0:
                    for s in range(lead):
                        scan(Sequence(0), s)
                step(Sequence(b))
            with engine.Fori(0, LOOP_END - LOOP_FIRST, LOOP_STEP) as register:
                for b in range(LOOP_FIRST, LOOP_FIRST + LOOP_STEP):
                    step(Sequence(b, register.with_bounds(max_val=LOOP_END - LOOP_FIRST - LOOP_STEP)))
            for b in range(LOOP_END, BATCH + 1):
                step(Sequence(b))

        loads, late = [], []

        @block.sync
        def _(sp):
            def load(dst, src):
                loads.append(1)
                sp.dma_start(dst, src).then_inc(weights_in, 16)

            def late_load(dst, src):
                late.append(1)
                sp.dma_start(dst, src).then_inc(experts_in, 16)

            with nc.allow_non_contiguous_dma(reason="a few columns of constants"):
                load(lnw_c[:, :], ln_w.rearrange("(c p) -> p c", p=P))
                load(lnb_c[:, :], ln_b.rearrange("(c p) -> p c", p=P))
                load(projb_c[:, :], proj_b.rearrange("(c p) -> p c", p=P))
                load(branchb_c[:, 0, :], f_b.rearrange("(c p) -> p c", p=P))
                load(branchb_c[:, 1, :], b_b.rearrange("(c p) -> p c", p=P))
                load(dtb_c[:, :], dt_b.rearrange("(c p) -> p c", p=P))
                load(d_c[:, :], D.rearrange("(c p) -> p c", p=P))
            load(neg_a[:, :, :], A_log.rearrange("(c p) n -> p c n", p=P))
            load(proj_sb[:, :, :], projT.rearrange("(c p) n -> p c n", p=P))
            load(branch_sb[:, 0, :, :], fT.rearrange("(c p) n -> p c n", p=P))
            load(branch_sb[:, 1, :, :], bT.rearrange("(c p) n -> p c n", p=P))
            dbc = dbcT.rearrange("(c p) n -> p c n", p=P)
            load(dbc_sb[:, :, 0:DT_RANK], dbc[:, :, 0:DT_RANK])
            load(dbc_sb[:, :, ROW_B:ROW_B + STATES], dbc[:, :, DT_RANK:DT_RANK + STATES])
            for row in (ROW_C, ROW_C2, ROW_C2 + STATES):
                load(dbc_sb[:, :, row:row + STATES], dbc[:, :, DT_RANK + STATES:DT_RANK + 2 * STATES])
            load(dt_sb[:, :], dtT)
            late_load(gate_sb[:, :, :], gateT.rearrange("(c p) n -> p c n", p=P))
            late_load(bias_sb[:, :], bias_e.partition_broadcast(P))
            late_load(sup_sb[:, :, :], shared_upT.rearrange("(c p) n -> p c n", p=P))
            late_load(sdown_sb[:, :, :], shared_downT.rearrange("(c p) n -> p c n", p=P))
            late_load(up_sb[:, :, :], upT.rearrange("(c p) n -> p c n", p=P))
            late_load(down_sb[:, :, :], downT.rearrange("e p n -> p e n"))

            def count(value):
                if not isinstance(value, int):
                    sp.compute_val(value)
                return value

            def load_b(b, n):
                used = count(b.times(UNITS * STATES, UNITS * (n - B_RING + 1)))
                stored = count((b + 1).times(16 * BRANCHES))
                if b > 0 or n >= B_RING:
                    sp.wait_ge(input_done, used)
                sp.wait_ge(b_stored, stored)
                sp.dma_start(b_ring[:, n % B_RING, :, :],
                             b_dram[b % 2, :, n, :].partition_broadcast(P)).then_inc(b_in[n % B_RING], 16)

            def prep(b, s):
                if s == B_STORE_SLOT:
                    for r in range(BRANCHES):
                        sp.wait_ge(ps.sem, ps.by(b, f"db{r}"))
                        sp.dma_start(b_dram[b % 2, r, :, :], low[ROW_B:ROW_B + STATES, r, :]).then_inc(b_stored, 16)
                if b.at == 0 and s == SLOTS - 1:
                    for n in range(B_RING - 1):
                        load_b(b, n)

            def scan(b, s):
                if s % 2 == 0:
                    n = s // 2 + B_RING - 1
                    if n < STATES:
                        load_b(b, n)
                    elif b.at + 1 < BATCH:
                        load_b(b + 1, n - STATES)

            def ffn(b, s):
                if s == CW_SLOT + 1:
                    sp.wait_ge(fs.sem, fs.by(b, "cwT"))
                    sp.dma_start(cw_dram[b % 2, :, :], cwT).then_inc(cw_stored, 16)
                for m in pairs_at(s, 0, experts_only=True):
                    half, k = m // PAIRS, m % PAIRS - SHARED_PAIRS
                    before = (half * EXPERT_PAIRS + k) - CW_RING
                    if b > 0 or before >= 0:
                        b_, i = (b, before) if before >= 0 else (b - 1, before + 2 * EXPERT_PAIRS)
                        last = f"weigh{(i // EXPERT_PAIRS) * PAIRS + SHARED_PAIRS + i % EXPERT_PAIRS}"
                        used, stored = count(fp.by(b_, last)), count((b + 1).times(16))
                        sp.wait_ge(fp.sem, used)
                    else:
                        stored = count((b + 1).times(16))
                    sp.wait_ge(cw_stored, stored)
                    sp.dma_start(cw_ring[:, k % CW_RING, :, :],
                                 cw_dram[b % 2, 2 * k:2 * k + 2, half * HALF:(half + 1) * HALF].partition_broadcast(P)
                                 ).then_inc(cw_in[k % CW_RING], 16)

            run(sp, lambda b, s: None, prep, scan, ffn)
            sp.wait_ge(out_stored, 16 * 2 * BATCH)

        WEIGHTS, EXPERT_WEIGHTS = 16 * len(loads), 16 * len(late)

        @block.gpsimd
        def _(pool):
            nc.gpsimd.memset(ident[:, :], 0.0).then_inc(pool_consts, 1)
            nc.gpsimd.memset(pick[:, :], 0.0).then_inc(pool_consts, 1)
            nc.gpsimd.memset(lower[:, :, :], 1.0).then_inc(pool_consts, 1)
            nc.gpsimd.memset(third[:, :], -1.0).then_inc(pool_consts, 1)
            nc.gpsimd.memset(c_parts[:, :, :, :], 0.0).then_inc(pool_consts, 1)
            pool.wait_ge(pool_consts, 5)
            nc.gpsimd.affine_select(out=ident[:, :], in_=ident[:, :], compare_op=ALU.not_equal, fill=1.0,
                                    base=0, pattern=[[-1, P]], channel_multiplier=1).then_inc(pool_consts, 1)
            nc.gpsimd.affine_select(out=lower[:, :, :], in_=lower[:, :, :], compare_op=ALU.is_gt, fill=0.0,
                                    base=0, pattern=[[1, GROUPS], [-1, GROUPS]], channel_multiplier=0
                                    ).then_inc(pool_consts, 1)
            nc.gpsimd.affine_select(out=third[:, :], in_=third[:, :], compare_op=ALU.is_ge, fill=0.0,
                                    base=-(ROW_C2 + STATES), pattern=[[0, 1]], channel_multiplier=1
                                    ).then_inc(pool_consts, 1)
            for part, row in enumerate((ROW_C, ROW_C2, ROW_C2 + STATES)):
                pool.wait_ge(pool_consts, 8 + part)
                nc.gpsimd.affine_select(out=pick[:, :], in_=pick[:, :], compare_op=ALU.not_equal, fill=1.0,
                                        base=-row, pattern=[[-1, STATES]], channel_multiplier=1
                                        ).then_inc(pool_consts, 1)

            def prep(b, s):
                if s == 0:
                    pool.wait_ge(ns.sem, ns.by(b, "xl"))
                    if b > 1:
                        pool.wait_ge(fve.sem, fve.by(b - 2, "x1"))
                    nc.gpsimd.tensor_tensor(xs[:, b % 2, :, :], x_sb[:, :, :], xl[:, :, :], ALU.add
                                            ).then_inc(*pp.inc("xs"))
                if s == Z_SLOTS[3]:
                    pool.wait_ge(ps.sem, ps.by(b, "z_sig"))
                    nc.gpsimd.tensor_tensor(z_sb, z_sb, xpT[:, :, :], ALU.mult).then_inc(*pp.inc("z"))
                for tag, j in softplus_at(s, LOWER):
                    dst = softplus_dst(b, tag, j)
                    pool.wait_ge(ps.sem, ps.by(b, f"{tag}_lin{j}"))
                    nc.gpsimd.tensor_tensor(dst, dst, ex[:, j, :], ALU.mult).then_inc(*pp.inc(f"{tag}_low{j}"))
                for tag, j in softplus_at(s, MAXIMUM + 1):
                    if tag == "d":
                        pool.wait_ge(pv.sem, pv.by(b, f"d{j}"))
                        if b > 1 and j == 0:
                            pool.wait_ge(input_done, (b - 1).times(UNITS * STATES))
                        nc.gpsimd.tensor_tensor(du[:, b % 2, j, :], delta[:, b % 2, j, :], u_sb[:, j, :], ALU.mult
                                                ).then_inc(*pp.inc(f"du{j}"))
                if s == UD_SLOT:
                    if b > 0:
                        pool.wait_ge(y_started, b.number())
                    if b > 1:
                        pool.wait_ge(cw_stored, (b - 1).times(16))
                    pool.wait_ge(pv.sem, pv.by(b, f"u{UNITS - 1}"))
                    nc.gpsimd.tensor_tensor(ud[:, :, :], u_sb[:, 0:CT, :], u_sb[:, CT:UNITS, :], ALU.add
                                            ).then_inc(*pp.inc("u_sum"))

            def ffn(b, s):
                for m in pairs_at(s, 2, experts_only=True):
                    half, k = m // PAIRS, m % PAIRS - SHARED_PAIRS
                    pool.wait_ge(fte.sem, fte.by(b, f"down{m - 2}"))
                    uses = half * (EXPERT_PAIRS // CW_RING) + k // CW_RING + 1
                    pool.wait_ge(cw_in[k % CW_RING], b.times(16 * (2 * EXPERT_PAIRS // CW_RING), 16 * uses))
                    pool.wait_ge(fs.sem, fs.by(b, f"square{m}"))
                    nc.gpsimd.tensor_tensor(hidden[:, m % 2, :, :], act_sb[:, m % 2, :, :],
                                            cw_ring[:, k % CW_RING, :, :], ALU.mult).then_inc(*fp.inc(f"weigh{m}"))

            def scan(b, s):
                n = s // 2
                for j in (2 * (s % 2), 2 * (s % 2) + 1):
                    g = n * UNITS + j
                    r = j // CT
                    if g == 0:
                        pool.wait_ge(pp.sem, pp.by(b, f"du{UNITS - 1}"))
                    if j == 0:
                        pool.wait_ge(b_in[n % B_RING], b.times(16 * (STATES // B_RING), 16 * (n // B_RING + 1)))
                    if b > 0 or g >= STATE_RING:
                        pool.wait_ge(y_added, b.times(STATES * UNITS, g - STATE_RING + 1))
                    nc.gpsimd.tensor_tensor(state[:, g % STATE_RING, :], du[:, b % 2, j, :],
                                            b_ring[:, n % B_RING, r, :], ALU.mult).then_inc(input_done, 1)

            run(pool, lambda b, s: None, prep, scan, ffn, lead=POOL_LEAD)

        @block.scalar
        def _(act):
            nc.scalar.preload_act_table_set("natural_log_exp_and_others")

            def load_x(b):
                if b > 0:
                    act.wait_ge(pt.sem, pt.by(b - 1, "xp1"))
                act.dma_start(x_sb[:, :, :], x[b.number(), :, :].rearrange("(t p) c -> p t c", p=P)).then_inc(x_in, 16)

            load_x(Sequence(0))

            def rsqrt_guess(b, steps, vsteps, tag, v, y):
                act.wait_ge(vsteps.sem, vsteps.by(b, f"{tag}_var"))
                nc.scalar.activation(y[:, :], v[:, :], ACT.Ln).then_inc(*steps.inc(f"{tag}_ln"))
                act.wait_ge(steps.sem, steps.by(b, f"{tag}_ln"))
                nc.scalar.activation(y[:, :], y[:, :], ACT.Exp, scale=-0.5).then_inc(*steps.inc(f"{tag}_y"))

            def magnitude(b, name, tag, j, bias):
                if tag == "u":
                    act.wait_ge(pt.sem, pt.by(b, "xnT1"))
                else:
                    act.wait_ge(pv.sem, pv.by(b, f"u_max{j}"))
                act.wait_ge(pt.sem, pt.by(b, name))
                nc.scalar.activation(ex[:, j, :], product_bank(b, name)[:, :], ACT.Abs, bias=bias
                                     ).then_inc(*ps.inc(f"abs_{name}"))

            def evacuate(b, name, dst, bias=0.0, scale=1.0, src=None):
                act.wait_ge(pt.sem, pt.by(b, name))
                nc.scalar.activation(dst, product_bank(b, name)[:, :] if src is None else src, ACT.Identity, bias=bias,
                                     scale=scale).then_inc(*ps.inc(name))

            def norm_apply(b, steps, vsteps, tag, dst, src, r_, bias, done):
                act.wait_ge(vsteps.sem, vsteps.by(b, f"{tag}_bias"))
                for t in range(TT):
                    last = nc.scalar.activation(dst[:, t, :], src[:, t, :], ACT.Identity, bias=bias[:, t:t + 1],
                                                scale=r_[:, t:t + 1])
                last.then_inc(*steps.inc(done))

            def norm(b, s):
                if s == NORM_SLOTS[1]:
                    rsqrt_guess(b, ns, nve, "outer", nv, ny)
                if s == NORM_SLOTS[3]:
                    if b > 0:
                        act.wait_ge(pt.sem, pt.by(b - 1, "zT1"))
                    norm_apply(b, ns, nve, "outer", xl, x_sb, nr, nb, "xl")
                if s == NORM_SLOTS[5]:
                    rsqrt_guess(b, ns, nve, "inner", nv, ny)
                if s == NORM_SLOTS[7]:
                    if b > 0:
                        act.wait_ge(pv.sem, pv.by(b - 1, f"d{UNITS - 1}"))
                    norm_apply(b, ns, nve, "inner", xn, xl, nr, nb, "xn")

            def copy_out(b, name):
                kind, j = name.rstrip("0123"), int(name[-1])
                c, r = j % CT, j // CT
                if kind == "xnT":
                    act.wait_ge(pp.sem, pp.by(b, "xs"))
                    evacuate(b, name, xnT[:, j, :], lnb_c[:, j:j + 1], lnw_c[:, j:j + 1])
                elif kind == "xp":
                    if b > 0:
                        act.wait_ge(pt.sem, pt.by(b - 1, "u3"))
                        act.wait_ge(pp.sem, pp.by(b - 1, "z"))
                    evacuate(b, name, xpT[:, j, :], projb_c[:, j:j + 1])
                elif kind == "u":
                    if b > 0 and j == 0:
                        act.wait_ge(pv.sem, pv.by(b - 1, f"d{UNITS - 1}"))
                    magnitude(b, name, "u", j, branchb_c[:, r, c:c + 1])
                    evacuate(b, name, pre[:, j, :], branchb_c[:, r, c:c + 1])
                elif kind == "zT":
                    if b > 1 and j == 0:
                        act.wait_ge(fve.sem, fve.by(b - 2, "yz1"))
                    evacuate(b, name, zT[:, b % 2, :, j * P:(j + 1) * P],
                             src=product_bank(b, name)[:, :].rearrange("p (t c) -> p t c", t=TT))
                elif kind == "db":
                    if b > 0 and j == 0:
                        act.wait_ge(b_stored, b.times(16 * BRANCHES))
                        act.wait_ge(pt.sem, pt.by(b - 1, "d3"))
                        act.wait_ge(ps.sem, ps.by(b - 1, "c_lo"))
                    evacuate(b, name, low[:, j, :])
                else:
                    act.wait_ge(pv.sem, pv.by(b, f"u{j}"))
                    magnitude(b, name, "d", j, dtb_c[:, c:c + 1])
                    evacuate(b, name, pre[:, j, :], dtb_c[:, c:c + 1])

            def prep(b, s):
                if b.at == 0 and s == 0:
                    act.wait_ge(weights_in, WEIGHTS)
                    nc.scalar.activation(neg_a[:, :, :], neg_a[:, :, :], ACT.Exp).then_inc(a_done, 1)
                    act.wait_ge(a_done, 1)
                    nc.scalar.activation(neg_a[:, :, :], neg_a[:, :, :], ACT.Identity, scale=-1.0).then_inc(a_done, 1)
                for name, at in PREP_PRODUCTS.items():
                    if at + 1 == s:
                        copy_out(b, name)
                if s == LOAD_SLOT and b.at + 1 < BATCH:
                    load_x(b + 1)
                if s == Z_SLOTS[0]:
                    act.wait_ge(ns.sem, ns.by(b, "xn"))
                    act.wait_ge(pp.sem, pp.by(b, "xs"))
                    act.wait_ge(ps.sem, ps.by(b, "xp1"))
                    nc.scalar.activation(z_sb, xpT[:, :, :], ACT.Exp, scale=-1.0).then_inc(*ps.inc("z_exp"))
                if s == Z_SLOTS[1]:
                    act.wait_ge(ps.sem, ps.by(b, "z_exp"))
                    nc.scalar.activation(z_sb, z_sb, ACT.Ln, bias=1.0).then_inc(*ps.inc("z_ln"))
                if s == Z_SLOTS[2]:
                    act.wait_ge(ps.sem, ps.by(b, "z_ln"))
                    nc.scalar.activation(z_sb, z_sb, ACT.Exp, scale=-1.0).then_inc(*ps.inc("z_sig"))
                for tag, j in softplus_at(s, EXPONENT):
                    act.wait_ge(ps.sem, ps.by(b, f"abs_{tag}{j}"))
                    nc.scalar.activation(ex[:, j, :], ex[:, j, :], ACT.Exp, scale=-1.0
                                         ).then_inc(*ps.inc(f"{tag}_exp{j}"))
                    if tag == "u" and j == 0 and b > 0:
                        act.wait_ge(pp.sem, pp.by(b - 1, "u_sum"))
                        act.wait_ge(pp.sem, pp.by(b - 1, f"du{UNITS - 1}"))
                        act.wait_ge(pt.sem, pt.by(b - 1, "db1"))
                    if tag == "d" and j == 0 and b > 1:
                        act.wait_ge(pp.sem, pp.by(b - 2, f"du{UNITS - 1}"))
                    act.wait_ge(ps.sem, ps.by(b, f"{tag}_exp{j}"))
                    nc.scalar.activation(softplus_dst(b, tag, j), ex[:, j, :], ACT.Identity, scale=-0.5, bias=1.0
                                         ).then_inc(*ps.inc(f"{tag}_lin{j}"))
                for tag, j in softplus_at(s, LOGARITHM):
                    act.wait_ge(pp.sem, pp.by(b, f"{tag}_low{j}"))
                    nc.scalar.activation(ex[:, j, :], ex[:, j, :], ACT.Ln, bias=1.0).then_inc(*ps.inc(f"{tag}_ln{j}"))
                if s == C_SPLIT_SLOT:
                    act.wait_ge(ps.sem, ps.by(b, "db1"))
                    if b > 1:
                        act.wait_ge(c_done, (b - 1).times(SLOTS))
                    else:
                        act.wait_ge(pool_consts, 11)
                    nc.scalar.activation(c_parts[ROW_C:P, b % 2, :, :], low[ROW_C:P, :, :], ACT.Identity
                                         ).then_inc(*ps.inc("c_hi"))
                for after, residue, name in ((1, "c_r1", "c_mid"), (2, "c_r2", "c_lo")):
                    if s == C_SPLIT_SLOT + after:
                        act.wait_ge(pv.sem, pv.by(b, residue))
                        nc.scalar.activation(c_parts[ROW_C2:P, b % 2, :, :], low[ROW_C2:P, :, :], ACT.Identity
                                             ).then_inc(*ps.inc(name))
                if s == UD_SLOT + 1:
                    act.wait_ge(pp.sem, pp.by(b, "u_sum"))
                    for c in range(CT):
                        last = nc.scalar.activation(ud[:, c, :], ud[:, c, :], ACT.Identity, scale=d_c[:, c:c + 1])
                    last.then_inc(*ps.inc("ud"))

            def scan(b, s):
                n = s // 2
                for j in (2 * (s % 2), 2 * (s % 2) + 1):
                    g = n * UNITS + j
                    if g == 0:
                        act.wait_ge(pv.sem, pv.by(b, f"d{UNITS - 1}"))
                        if b.at == 0:
                            act.wait_ge(a_done, 2)
                    if b > 0 or g >= 2:
                        act.wait_ge(scan_done, b.times(STATES * UNITS, g - 1))
                    nc.scalar.activation(decay[g % 2][:, :], delta[:, b % 2, j, :], ACT.Exp,
                                         scale=neg_a[:, j % CT, n:n + 1]).then_inc(decay_done, 1)

            def ffn(b, s):
                if s == HEAD_SLOTS[1]:
                    rsqrt_guess(b, fs, fve, "ffn", fv, fy)
                if s == HEAD_SLOTS[3]:
                    if b > 0:
                        act.wait_ge(fp.sem, fp.by(b - 1, f"weigh{2 * PAIRS - 1}"))
                    norm_apply(b, fs, fve, "ffn", xf, x1, fr, fb, "xf")
                for c in [c for c in range(CT) if XFT_SLOTS[c] + 1 == s]:
                    act.wait_ge(fte.sem, fte.by(b, f"xfT{c}"))
                    if b > 0 and c == 0:
                        act.wait_ge(fte.sem, fte.by(b - 1, f"up{2 * PAIRS - 1}"))
                    nc.scalar.activation(xfT[:, c, :], ffn_bank[:, :], ACT.Identity).then_inc(*fs.inc(f"xfT{c}"))
                if s == LOGITS_SLOT + 1:
                    act.wait_ge(fte.sem, fte.by(b, "logits"))
                    nc.scalar.activation(r_e[:, :], ffn_bank[:, 0:TE], ACT.Exp, scale=-1.0
                                         ).then_inc(*fs.inc("z_logits"))
                if s == CW_SLOT + 1:
                    act.wait_ge(fte.sem, fte.by(b, "cwT"))
                    act.wait_ge(y_started, (b + 2 if b.at + 2 <= BATCH else b + 1).number())
                    nc.scalar.activation(cwT, ffn_bank[0:EXPERTS, :], ACT.Identity).then_inc(*fs.inc("cwT"))
                for m in pairs_at(s, 1):
                    if m >= 2 and is_expert(m - 2):
                        act.wait_ge(fp.sem, fp.by(b, f"weigh{m - 2}"))
                    elif m >= 2:
                        act.wait_ge(fs.sem, fs.by(b, f"square{m - 2}"))
                    elif m < 2 and b > 0:
                        act.wait_ge(fp.sem, fp.by(b - 1, f"weigh{2 * PAIRS - 2 + m}"))
                    act.wait_ge(fte.sem, fte.by(b, f"up{m}"))
                    a = act_sb[:, m % 2, :, :].rearrange("p a b -> p (a b)")
                    nc.scalar.activation(a, up_bank(b, m)[:, :], ACT.Relu).then_inc(*fs.inc(f"relu{m}"))
                    if is_expert(m):
                        act.wait_ge(fs.sem, fs.by(b, f"relu{m}"))
                        nc.scalar.activation(a, a, ACT.Square).then_inc(*fs.inc(f"square{m}"))
                for m in pairs_at(s, 2):
                    if not is_expert(m):
                        if m >= 2:
                            act.wait_ge(fte.sem, fte.by(b, f"down{m - 2}"))
                        elif b > 0:
                            act.wait_ge(fte.sem, fte.by(b - 1, f"down{2 * PAIRS - 2 + m}"))
                        act.wait_ge(fs.sem, fs.by(b, f"relu{m}"))
                        nc.scalar.activation(hidden[:, m % 2, :, :], act_sb[:, m % 2, :, :], ACT.Square
                                             ).then_inc(*fs.inc(f"square{m}"))
                if s == OUT_SLOT[0] + 1:
                    store(b, 0)
                if s == 0 and b > 0:
                    store(b - 1, 1)

            def store(b, half):
                act.wait_ge(fve.sem, fve.by(b, f"out{half}"))
                act.dma_start(out[b.number(), half * HALF:(half + 1) * HALF, :].rearrange("(t p) c -> p t c", p=P),
                              out_sb[:, :, :]).then_inc(out_stored, 16)

            run(act, norm, prep, scan, ffn)
            store(Sequence(BATCH - 1), 1)

        @block.vector
        def _(dve):
            nc.vector.memset(restart[:, :], 1.0).then_inc(vector_consts, 1)
            dve.wait_ge(vector_consts, 1)
            nc.vector.memset(restart[:, :].rearrange("p (t e) -> p t e", e=EXPERTS)[:, :, 0:1], 0.0
                             ).then_inc(vector_consts, 1)
            dve.wait_ge(pool_consts, 11)
            dve.wait_ge(vector_consts, 2)

            def carry_wait():
                nc.vector.memset(carrier[:, :], 0.0)

            def norm_moments(b, steps, tag, src, st, m, v):
                for t in range(TT):
                    last = nc.vector.bn_stats(st[:, t, :], src[:, t, :])
                last.then_inc(*steps.inc(f"{tag}_stats"))
                dve.wait_ge(steps.sem, steps.by(b, f"{tag}_stats"))
                carry_wait()
                for t in range(TT):
                    last = nc.vector.bn_aggr(m[:, t, :], st[:, t, :])
                last.then_inc(*steps.inc(f"{tag}_moments"))
                dve.wait_ge(steps.sem, steps.by(b, f"{tag}_moments"))
                nc.vector.tensor_scalar(v[:, :], m[:, :, 1], EPS, None, ALU.add).then_inc(*steps.inc(f"{tag}_var"))

            def newton(b, steps, ssteps, tag, m, v, y, t_, r_, bias):
                dve.wait_ge(ssteps.sem, ssteps.by(b, f"{tag}_y"))
                nc.vector.tensor_tensor(t_[:, :], y[:, :], y[:, :], ALU.mult).then_inc(*steps.inc(f"{tag}_y2"))
                dve.wait_ge(steps.sem, steps.by(b, f"{tag}_y2"))
                nc.vector.tensor_tensor(t_[:, :], t_[:, :], v[:, :], ALU.mult).then_inc(*steps.inc(f"{tag}_vy2"))
                dve.wait_ge(steps.sem, steps.by(b, f"{tag}_vy2"))
                nc.vector.tensor_scalar(t_[:, :], t_[:, :], -0.5, 1.5, ALU.mult, ALU.add
                                        ).then_inc(*steps.inc(f"{tag}_corr"))
                dve.wait_ge(steps.sem, steps.by(b, f"{tag}_corr"))
                nc.vector.tensor_tensor(r_[:, :], y[:, :], t_[:, :], ALU.mult).then_inc(*steps.inc(f"{tag}_rstd"))
                dve.wait_ge(steps.sem, steps.by(b, f"{tag}_rstd"))
                nc.vector.scalar_tensor_tensor(bias[:, :], m[:, :, 0], -1.0, r_[:, :], ALU.mult, ALU.mult
                                               ).then_inc(*steps.inc(f"{tag}_bias"))

            def norm(b, s):
                if s == NORM_SLOTS[0]:
                    dve.wait_ge(x_in, (b + 1).times(16))
                    norm_moments(b, nve, "outer", x_sb, stats, mv, nv)
                if s == NORM_SLOTS[2]:
                    newton(b, nve, ns, "outer", mv, nv, ny, nt, nr, nb)
                if s == NORM_SLOTS[4]:
                    dve.wait_ge(ns.sem, ns.by(b, "xl"))
                    norm_moments(b, nve, "inner", xl, stats, mv, nv)
                if s == NORM_SLOTS[6]:
                    newton(b, nve, ns, "inner", mv, nv, ny, nt, nr, nb)

            def prep(b, s):
                for tag, j in softplus_at(s, MAXIMUM):
                    dst = u_sb[:, j, :] if tag == "u" else delta[:, b % 2, j, :]
                    dve.wait_ge(ps.sem, ps.by(b, f"{tag}_ln{j}"))
                    nc.vector.tensor_tensor(dst, dst, ex[:, j, :], ALU.max).then_inc(*pv.inc(f"{tag}_max{j}"))
                    dve.wait_ge(pv.sem, pv.by(b, f"{tag}_max{j}"))
                    nc.vector.scalar_tensor_tensor(dst, pre[:, j, :], 0.0, dst, ALU.max, ALU.add
                                                   ).then_inc(*pv.inc(f"{tag}{j}"))
                rest, part = low[ROW_C2:P, :, :], c_parts[ROW_C2:P, b % 2, :, :]
                if s == C_SPLIT_SLOT:
                    dve.wait_ge(ps.sem, ps.by(b, "c_hi"))
                    nc.vector.tensor_tensor(rest, rest, part, ALU.subtract).then_inc(*pv.inc("c_r1"))
                if s == C_SPLIT_SLOT + 1:
                    dve.wait_ge(ps.sem, ps.by(b, "c_mid"))
                    nc.vector.scalar_tensor_tensor(rest, part, third[ROW_C2:P, :], rest, ALU.mult, ALU.add
                                                   ).then_inc(*pv.inc("c_r2"))

            def scan(b, s):
                n = s // 2
                pair = (2 * (s % 2), 2 * (s % 2) + 1)
                for j in pair:
                    g = n * UNITS + j
                    dve.wait_ge(decay_done, b.times(STATES * UNITS, g + 1))
                    dve.wait_ge(input_done, b.times(STATES * UNITS, g + 1))
                    slot = state[:, g % STATE_RING, :]
                    nc.vector.tensor_tensor_scan(slot, decay[g % 2][:, :], slot, 0.0, ALU.mult, ALU.add
                                                 ).then_inc(scan_done, 1)
                for j in pair:
                    g = n * UNITS + j
                    if j % CT == 0:
                        dve.wait_ge(c_done, b.times(STATES * BRANCHES, n * BRANCHES + j // CT + 1))
                    dve.wait_ge(scan_done, b.times(STATES * UNITS, g + 1))
                    slot = state[:, g % STATE_RING, :]
                    nc.vector.tensor_tensor(slot, slot, c_bank_of(s)[:, :], ALU.mult).then_inc(yc_done, 1)

            def te(tile):
                return tile[:, :].rearrange("p (t e) -> p t e", e=EXPERTS)

            tt_ = nc.vector.tensor_tensor

            def chain(b, part):
                at = [0]

                def link(ins):
                    ins.then_inc(*fve.inc(f"route{part}_{at[0]}"))
                    dve.wait_ge(fve.sem, fve.by(b, f"route{part}_{at[0]}"))
                    at[0] += 1

                return link

            def route_scores(b, link):
                if b.at == 0:
                    dve.wait_ge(experts_in, EXPERT_WEIGHTS)
                dve.wait_ge(fs.sem, fs.by(b, "z_logits"))
                link(nc.vector.tensor_scalar(r_e[:, :], r_e[:, :], 1.0, None, ALU.add))
                link(nc.vector.reciprocal(r_s[:, :], r_e[:, :]))
                link(tt_(te(r_b), te(r_s), bias_sb[:, :].unsqueeze(1).to_broadcast([P, TT, EXPERTS]), ALU.add))
                two = r_b[:, :].rearrange("p (a b) -> p a b", b=2)
                tt_(r_hi[:, :], two[:, :, 0], two[:, :, 1], ALU.max)
                link(tt_(r_lo[:, :], two[:, :, 0], two[:, :, 1], ALU.min))
                hi = r_hi[:, :].rearrange("p (a b) -> p a b", b=2)
                lo = r_lo[:, :].rearrange("p (a b) -> p a b", b=2)
                tt_(r_gs[:, :], hi[:, :, 0], hi[:, :, 1], ALU.max)
                tt_(r_t1[:, :], hi[:, :, 0], hi[:, :, 1], ALU.min)
                link(tt_(r_t2[:, :], lo[:, :, 0], lo[:, :, 1], ALU.max))
                link(tt_(r_t1[:, :], r_t1[:, :], r_t2[:, :], ALU.max))
                link(tt_(r_gs[:, :], r_gs[:, :], r_t1[:, :], ALU.add))

            def route_groups(b, link):
                gs = r_gs[:, :].rearrange("p (t g) -> p t g", g=GROUPS)
                shape = [P, TT, GROUPS, GROUPS]
                own, other = gs.unsqueeze(3).to_broadcast(shape), gs.unsqueeze(2).to_broadcast(shape)
                tt_(r_c1[:, :, :, :], other, own, ALU.is_gt)
                link(tt_(r_c2[:, :, :, :], other, own, ALU.is_equal))
                link(tt_(r_c2[:, :, :, :], r_c2[:, :, :, :], lower[:, :, :].unsqueeze(1).to_broadcast(shape), ALU.mult))
                link(tt_(r_c1[:, :, :, :], r_c1[:, :, :, :], r_c2[:, :, :, :], ALU.add))
                link(nc.vector.tensor_reduce(r_gk[:, :], r_c1[:, :, :, :].rearrange("p t g h -> p (t g) h"), AX.X, ALU.add))
                link(nc.vector.tensor_scalar(r_gk[:, :], r_gk[:, :], float(TOP_GROUPS), None, ALU.is_lt))
                per = EXPERTS // GROUPS
                link(tt_(r_m[:, :].rearrange("p (g k) -> p g k", k=per), r_b[:, :].rearrange("p (g k) -> p g k", k=per),
                         r_gk[:, :].unsqueeze(2).to_broadcast([P, TT * GROUPS, per]), ALU.mult))

            def route_experts(b, link):
                carry_wait()
                for t in range(TT):
                    last = nc.vector.max(r_top[:, t, :], te(r_m)[:, t, :])
                link(last)
                fourth = r_top[:, :, TOP_K - 1:TOP_K].to_broadcast([P, TT, EXPERTS])
                tt_(te(r_g), te(r_m), fourth, ALU.is_gt)
                link(tt_(te(r_q), te(r_m), fourth, ALU.is_equal))
                link(nc.vector.tensor_reduce(r_n[:, :], te(r_g), AX.X, ALU.add))
                link(nc.vector.tensor_scalar(r_n[:, :], r_n[:, :], -1.0, float(TOP_K), ALU.mult, ALU.add))
                link(nc.vector.tensor_tensor_scan(r_m[:, :], restart[:, :], r_q[:, :], 0.0, ALU.mult, ALU.add))
                link(tt_(te(r_m), te(r_m), r_n[:, :].unsqueeze(2).to_broadcast([P, TT, EXPERTS]), ALU.is_le))
                link(tt_(r_q[:, :], r_q[:, :], r_m[:, :], ALU.mult))
                link(tt_(r_g[:, :], r_g[:, :], r_q[:, :], ALU.add))

            def route_weights(b, link):
                link(tt_(r_w[:, :], r_s[:, :], r_g[:, :], ALU.mult))
                link(nc.vector.tensor_reduce(r_sum[:, :], te(r_w), AX.X, ALU.add))
                link(nc.vector.tensor_scalar(r_sum[:, :], r_sum[:, :], 1e-20, None, ALU.add))
                link(nc.vector.reciprocal(r_sum[:, :], r_sum[:, :]))
                link(nc.vector.scalar_tensor_tensor(te(r_w), te(r_w), ROUTED_SCALE,
                                                    r_sum[:, :].unsqueeze(2).to_broadcast([P, TT, EXPERTS]),
                                                    ALU.mult, ALU.mult))

            def ffn(b, s):
                if s == 0:
                    dve.wait_ge(y_added, (b + 1).times(UNITS * STATES))
                    if b > 0:
                        dve.wait_ge(fve.sem, fve.by(b - 1, "out1"))
                    for h in range(2):
                        nc.vector.tensor_tensor(x1[:, 2 * h:2 * h + 2, :], zT[:, b % 2, 2 * h:2 * h + 2, :],
                                                y_bank[h][:, :].rearrange("p (t c) -> p t c", t=2), ALU.mult
                                                ).then_inc(*fve.inc(f"yz{h}"))
                if s == HEAD_SLOTS[0]:
                    dve.wait_ge(fve.sem, fve.by(b, "yz1"))
                    dve.wait_ge(pp.sem, pp.by(b, "xs"))
                    nc.vector.tensor_tensor(x1[:, :, :], x1[:, :, :], xs[:, b % 2, :, :], ALU.add
                                            ).then_inc(*fve.inc("x1"))
                    dve.wait_ge(fve.sem, fve.by(b, "x1"))
                    norm_moments(b, fve, "ffn", x1, fstats, fmv, fv)
                if s == HEAD_SLOTS[2]:
                    newton(b, fve, fs, "ffn", fmv, fv, fy, ft, fr, fb)
                for part, stage in enumerate((route_scores, route_groups, route_experts, route_weights)):
                    if s == ROUTE_SLOTS[part]:
                        stage(b, chain(b, part))
                for half in range(2):
                    if OUT_SLOT[half] == s:
                        dve.wait_ge(fte.sem, fte.by(b, f"down{(half + 1) * PAIRS - 1}"))
                        if b > 0 or half > 0:
                            dve.wait_ge(out_stored, b.times(32, 16 * half))
                        nc.vector.tensor_tensor(out_sb[:, :, :], x1[:, 2 * half:2 * half + 2, :],
                                                down_bank[:, :].rearrange("p (t c) -> p t c", t=2), ALU.add
                                                ).then_inc(*fve.inc(f"out{half}"))

            run(dve, norm, prep, scan, ffn)

        @block.tensor
        def _(pe):
            pe.wait_ge(weights_in, WEIGHTS)
            pe.wait_ge(pool_consts, 11)

            def prep_free(b, name):
                i = PREP_TENSOR.index(name)
                back = 2 if b.at == 0 else 1
                if i >= back:
                    pe.wait_ge(ps.sem, ps.by(b, PREP_TENSOR[i - back]))
                elif b > 0:
                    pe.wait_ge(ps.sem, ps.by(b - 1, PREP_TENSOR[-1]))

            def transposes(bank_, src, name, steps):
                for t in range(TT):
                    last = nc.tensor.transpose(bank_[:, t * P:(t + 1) * P], src(t), ident[:, :])
                last.then_inc(*steps.inc(name))

            def product(bank_, lhsT, rhs, name):
                for k in range(CT):
                    last = nc.tensor.matmul(bank_[:, :], lhsT(k), rhs(k), start=(k == 0), stop=(k == CT - 1))
                last.then_inc(*pt.inc(name))

            def prep(b, s):
                for name, at in PREP_PRODUCTS.items():
                    if at == s:
                        prep_free(b, name)
                        prep_product(b, name)

            def prep_product(b, name):
                kind, j = name.rstrip("0123"), int(name[-1])
                c, r = j % CT, j // CT
                bank_ = product_bank(b, name)
                if kind == "xnT":
                    pe.wait_ge(ns.sem, ns.by(b, "xn"))
                    transposes(bank_, lambda t: xn[:, t, j * P:(j + 1) * P], name, pt)
                elif kind == "xp":
                    pe.wait_ge(ps.sem, ps.by(b, "xnT1"))
                    product(bank_, lambda k: proj_sb[:, k, j * P:(j + 1) * P], lambda k: xnT[:, k, :], name)
                elif kind == "u":
                    pe.wait_ge(ps.sem, ps.by(b, "xp1"))
                    product(bank_, lambda k: branch_sb[:, r, k, c * P:(c + 1) * P], lambda k: xpT[:, k, :], name)
                elif kind == "zT":
                    pe.wait_ge(pp.sem, pp.by(b, "z"))
                    transposes(bank_, lambda t: z_sb[:, j, t * P:(t + 1) * P], name, pt)
                elif kind == "db":
                    pe.wait_ge(pv.sem, pv.by(b, f"u{j * CT + CT - 1}"))
                    product(bank_, lambda k: dbc_sb[:, k, :], lambda k: u_sb[:, j * CT + k, :], name)
                else:
                    pe.wait_ge(ps.sem, ps.by(b, f"db{r}"))
                    nc.tensor.matmul(bank_[:, :], dt_sb[:, c * P:(c + 1) * P], low[0:DT_RANK, r, :],
                                     start=True, stop=True).then_inc(*pt.inc(name))
            def add_transposed(src, c, first, last_unit):
                for t in range(TT):
                    col = (t % 2) * DIM + c * P
                    last = nc.tensor.matmul(y_bank[t // 2][:, col:col + P], src(t), ident[:, :],
                                            start=first and t % 2 == 0, stop=last_unit,
                                            is_transpose=True, skip_group_check=True)
                return last

            def broadcast_c(b, s):
                n, r = s // 2, s % 2
                if s == 0:
                    pe.wait_ge(ps.sem, ps.by(b, "c_lo"))
                if s == 1 and ONE_C_BANK > 1:
                    if b > 1:
                        pe.wait_ge(fve.sem, fve.by(b - 2, "out1"))
                    elif b.at == 0:
                        pe.wait_ge(ps.sem, ps.by(b, PREP_TENSOR[-1]))
                elif b > 0 or s > 0:
                    pe.wait_ge(yc_done, b.times(STATES * UNITS, (s - (1 if 0 < s <= ONE_C_BANK else 0)) * CT))
                nc.tensor.matmul(c_bank_of(s)[:, :], pick[:, n:n + 1].to_broadcast([P, P]),
                                 c_parts[:, b % 2, r, :], start=True, stop=True).then_inc(c_done, 1)

            def scan(b, s):
                n, r = s // 2, s % 2
                if s == 0:
                    if b.at == 0:
                        broadcast_c(b, 0)
                    pe.wait_ge(ps.sem, ps.by(b, "ud"))
                    if b > 0:
                        pe.wait_ge(fve.sem, fve.by(b - 1, "yz1"))
                    for c in range(CT):
                        last = add_transposed(lambda t, c=c: ud[:, c, t * P:(t + 1) * P], c, c == 0, False)
                    last.then_inc(y_started, 1)
                if s == 0 and ONE_C_BANK > 1:
                    broadcast_c(b, 1)
                if s < ONE_C_BANK - 1:
                    broadcast_c(b, s + 2)
                elif ONE_C_BANK <= s < SLOTS - 1:
                    broadcast_c(b, s + 1)
                elif s == SLOTS - 1 and b.at + 1 < BATCH:
                    broadcast_c(b + 1, 0)
                for c in range(CT):
                    g = n * UNITS + r * CT + c
                    pe.wait_ge(yc_done, b.times(STATES * UNITS, g + 1))
                    add_transposed(lambda t: state[:, g % STATE_RING, t * P:(t + 1) * P], c, False,
                                   s == SLOTS - 1).then_inc(y_added, 1)

            def ffn(b, s):
                for c in [c for c in range(CT) if XFT_SLOTS[c] == s]:
                    pe.wait_ge(fs.sem, fs.by(b, "xf"))
                    if c > 0:
                        pe.wait_ge(fs.sem, fs.by(b, "xfT0"))
                    elif b > 0:
                        pe.wait_ge(fs.sem, fs.by(b - 1, f"relu{2 * PAIRS - 1}"))
                    transposes(ffn_bank, lambda t: xf[:, t, c * P:(c + 1) * P], f"xfT{c}", fte)
                if s == LOGITS_SLOT:
                    if b.at == 0:
                        pe.wait_ge(experts_in, EXPERT_WEIGHTS)
                    pe.wait_ge(fs.sem, fs.by(b, "xfT1"))
                    for t in range(TT):
                        for k in range(CT):
                            last = nc.tensor.matmul(ffn_bank[:, t * EXPERTS:(t + 1) * EXPERTS],
                                                    xfT[:, k, t * P:(t + 1) * P], gate_sb[:, k, :],
                                                    start=(k == 0), stop=(k == CT - 1))
                    last.then_inc(*fte.inc("logits"))
                if s == CW_SLOT:
                    pe.wait_ge(fve.sem, fve.by(b, f"route3_{ROUTE_STEPS[3] - 1}"))
                    pe.wait_ge(fs.sem, fs.by(b, "relu1"))
                    for t in range(TT):
                        last = nc.tensor.transpose(ffn_bank[0:EXPERTS, t * P:(t + 1) * P],
                                                   r_w[:, t * EXPERTS:(t + 1) * EXPERTS], ident[:, :])
                    last.then_inc(*fte.inc("cwT"))
                for m in pairs_at(s, 0):
                    if up_bank(b, 1) is prep_bank and m == 1:
                        pe.wait_ge(ps.sem, ps.by(b, PREP_TENSOR[-1]))
                    elif m in (0, 2):
                        pe.wait_ge(fs.sem, fs.by(b, "z_logits" if m == 0 else "cwT"))
                    else:
                        pe.wait_ge(fs.sem, fs.by(b, f"relu{m - (2 if up_bank(b, 1) is prep_bank else 1)}"))
                    half, q = m // PAIRS, m % PAIRS
                    for j in range(2):
                        for k in range(CT):
                            if q < SHARED_PAIRS:
                                w = sup_sb[:, k, (2 * q + j) * P:(2 * q + j + 1) * P]
                            else:
                                e = 2 * (q - SHARED_PAIRS) + j
                                w = up_sb[:, k, e * INTER:(e + 1) * INTER]
                            last = nc.tensor.matmul(up_bank(b, m)[:, j * HALF:(j + 1) * HALF], w,
                                                    xfT[:, k, half * HALF:(half + 1) * HALF],
                                                    start=(k == 0), stop=(k == CT - 1))
                    last.then_inc(*fte.inc(f"up{m}"))
                for m in downs_at(s):
                    half, q = m // PAIRS, m % PAIRS
                    if q < SHARED_PAIRS:
                        pe.wait_ge(fs.sem, fs.by(b, f"square{m}"))
                    else:
                        pe.wait_ge(fp.sem, fp.by(b, f"weigh{m}"))
                    if q == 0:
                        if half > 0:
                            pe.wait_ge(fve.sem, fve.by(b, "out0"))
                        elif b > 0:
                            pe.wait_ge(fve.sem, fve.by(b - 1, "out1"))
                        if half == 0 and ONE_C_BANK > 1 and b.at + 1 < BATCH:
                            pe.wait_ge(yc_done, (b + 1).times(STATES * UNITS, ONE_C_BANK * CT))
                    for j in range(2):
                        w = sdown_sb[:, 2 * q + j, :] if q < SHARED_PAIRS else down_sb[:, 2 * (q - SHARED_PAIRS) + j, :]
                        for t in range(2):
                            last = nc.tensor.matmul(down_bank[:, t * DIM:(t + 1) * DIM],
                                                    hidden[:, m % 2, j, t * P:(t + 1) * P], w,
                                                    start=(q == 0 and j == 0 and t == 0),
                                                    stop=(q == PAIRS - 1 and j == 1), skip_group_check=True)
                    last.then_inc(*fte.inc(f"down{m}"))

            run(pe, lambda b, s: None, prep, scan, ffn, scan_last=True)


_OUT = (BATCH, SEQ, DIM)


def kernel(**inputs):
    import numpy as np
    import concourse.bacc as bacc
    from concourse.bass_utils import run_bass_kernel_spmd

    def t(a):
        return np.ascontiguousarray(np.swapaxes(a, -1, -2))

    g = {k: np.asarray(v) for k, v in inputs.items()}
    A, F = "L0_attn_", "L0_ffn_"
    up = g[F + "up_w"]
    arrays = {
        "x": g[A + "x"], "ln_w": g[A + "ln_w"], "ln_b": g[A + "ln_b"],
        "projT": t(g[A + "proj_W"]), "proj_b": g[A + "proj_b"],
        "fT": t(g[A + "fconv_W"]), "f_b": g[A + "fconv_b"],
        "bT": t(g[A + "bconv_W"]), "b_b": g[A + "bconv_b"],
        "dbcT": t(g[A + "deltaBC_W"]), "dtT": t(g[A + "dt_W"]), "dt_b": g[A + "dt_b"],
        "A_log": g[A + "A_log"], "D": g[A + "D"],
        "gateT": t(g[F + "gate_w"]), "bias_e": g[F + "bias_e"],
        "upT": t(up.reshape(EXPERTS * INTER, DIM)), "downT": t(g[F + "down_w"]),
        "shared_upT": t(g[F + "shared_up"]), "shared_downT": t(g[F + "shared_down"]),
    }
    nc = bacc.Bacc("TRN2", target_bir_lowering=False, num_devices=1)
    args, data = [], {}
    for name, a in arrays.items():
        a = np.ascontiguousarray(a)
        data[f"{name}_dram"] = a
        args.append(nc.dram_tensor(f"{name}_dram", a.shape, mybir.dt.from_np(a.dtype), kind="ExternalInput").ap())
    args.append(nc.dram_tensor("out_dram", _OUT, mybir.dt.float32, kind="ExternalOutput").ap())
    block_kernel(nc, *args)
    r = run_bass_kernel_spmd(nc, [data], core_ids=[0])
    return r.results[0]["out_dram"]
```
